# Optimizing a Trainium2 kernel written in Bass

```python
import numpy as np
import jax
import jax.numpy as jnp

def _softmax(x, axis=-1):
    return jax.nn.softmax(x, axis=axis)

def _gelu(x):
    return jax.nn.gelu(x, approximate=True)

def _silu(x):
    return jax.nn.silu(x)

def _sigmoid(x):
    return jax.nn.sigmoid(x)

def _layernorm(x, axis=-1, eps=1e-05):
    m = jnp.mean(x, axis=axis, keepdims=True)
    v = jnp.var(x, axis=axis, keepdims=True)
    return (x - m) / jnp.sqrt(v + eps)

def _scatter_add(tgt, idx, src, axis=0):
    return tgt.at[idx].add(src)

def _segment_sum(src, seg, n):
    return jax.ops.segment_sum(src, seg, n)
kernel_name = 'mk_prb_d2_jaxref_r8_89f004'

def setup_inputs(seed: int=0):
    np.random.seed(seed)
    _w = jnp.asarray

    def _L0_attn_setup():
        import jax, jax.numpy as jnp
        import numpy as np
        DIM = 128
        N_HEADS = 16
        HEAD_DIM = DIM // N_HEADS
        SCALE = HEAD_DIM ** (-0.5)
        key = jax.random.key(seed)
        kx, kq, kk, kv = jax.random.split(key, 4)
        x = jax.random.normal(kx, (2, 256, DIM), dtype=jnp.float32)
        bv_q = jax.random.normal(kq, (N_HEADS, HEAD_DIM), dtype=jnp.float32) * 0.02
        bv_k = jax.random.normal(kk, (N_HEADS, HEAD_DIM), dtype=jnp.float32) * 0.02
        bv_v = jax.random.normal(kv, (N_HEADS, HEAD_DIM), dtype=jnp.float32) * 0.02
        return {'x': x, 'bv_q': bv_q, 'bv_k': bv_k, 'bv_v': bv_v}
    _L0_attn_in = _L0_attn_setup()

    def _L0_ffn_setup():
        import jax, jax.numpy as jnp
        import numpy as np
        DIM = 128
        INTER = 64
        E = 32
        TOPK = 4
        GROUPS = 8
        TOPK_GROUPS = 4
        SHARED_INTER = 2 * INTER
        ROUTE_SCALE = 1.0
        B, S = (8, 512)

        def _gate(xf, gw, gb):
            T = xf.shape[0]
            scores = jax.nn.softmax((xf @ gw + gb).astype(jnp.float32), axis=-1)
            original_scores = scores
            scores_g = scores.reshape(T, GROUPS, E // GROUPS)
            group_scores = jnp.sum(jax.lax.top_k(scores_g, 2)[0], axis=-1)
            gidx = jax.lax.top_k(group_scores, TOPK_GROUPS)[1]
            keep = jnp.zeros((T, GROUPS), bool).at[jnp.arange(T)[:, None], gidx].set(True)
            masked = jnp.where(keep[:, :, None], scores_g, -jnp.inf).reshape(T, E)
            indices = jax.lax.top_k(masked, TOPK)[1]
            weights = jnp.take_along_axis(original_scores, indices, axis=1) * ROUTE_SCALE
            return (weights.astype(xf.dtype), indices)
        key = jax.random.key(seed)
        ks = jax.random.split(key, 16)

        def xav(k, shape):
            fan_in, fan_out = (shape[-2], shape[-1])
            lim = np.sqrt(6.0 / (fan_in + fan_out))
            return jax.random.uniform(k, shape, jnp.float32, -lim, lim)
        return {'x': jax.random.normal(ks[0], (B, S, DIM), jnp.float32), 'gw': xav(ks[1], (DIM, E)), 'gb': jnp.zeros((E,), jnp.float32), 'w1': xav(ks[2], (E, DIM, INTER)), 'b1': jnp.zeros((E, INTER), jnp.float32), 'w3': xav(ks[3], (E, DIM, INTER)), 'b3': jnp.zeros((E, INTER), jnp.float32), 'w2': xav(ks[4], (E, INTER, DIM)), 'b2': jnp.zeros((E, DIM), jnp.float32), 'sw1': xav(ks[5], (DIM, SHARED_INTER)), 'sb1': jnp.zeros((SHARED_INTER,), jnp.float32), 'sw3': xav(ks[6], (DIM, SHARED_INTER)), 'sb3': jnp.zeros((SHARED_INTER,), jnp.float32), 'sw2': xav(ks[7], (SHARED_INTER, DIM)), 'sb2': jnp.zeros((DIM,), jnp.float32)}
    _L0_ffn_in = _L0_ffn_setup()

    def _L1_attn_setup():
        import jax, jax.numpy as jnp
        import numpy as np
        N_HEAD = 16
        POS_EMB_RADIUS = 128
        EMB = 128
        key = jax.random.key(seed)
        ks = jax.random.split(key, 6)
        B, S, E = (2, 256, EMB)
        hd = E // N_HEAD
        x = jax.random.normal(ks[0], (B, S, E), dtype=jnp.float32)
        pos_emb_k = jax.random.normal(ks[1], (2 * POS_EMB_RADIUS, hd), dtype=jnp.float32) * 0.02
        scale = 1.0 / np.sqrt(E)
        Wq = jax.random.normal(ks[2], (E, E), dtype=jnp.float32) * scale
        Wk = jax.random.normal(ks[3], (E, E), dtype=jnp.float32) * scale
        Wv = jax.random.normal(ks[4], (E, E), dtype=jnp.float32) * scale
        Wproj = jax.random.normal(ks[5], (E, E), dtype=jnp.float32) * scale
        return {'x': x, 'pos_emb_k': pos_emb_k, 'Wq': Wq, 'Wk': Wk, 'Wv': Wv, 'Wproj': Wproj}
    _L1_attn_in = _L1_attn_setup()

    def _L1_ffn_setup():
        import jax, jax.numpy as jnp
        import numpy as np
        E = 16
        K = 4
        G = 4
        TG = 2
        NS = 2
        H = 128
        I = 176
        SCALE = 1.0

        def _gate(x2d, gate_w, gate_bias):
            T = x2d.shape[0]
            logits = x2d.astype(jnp.float32) @ gate_w.astype(jnp.float32).T
            scores = jax.nn.sigmoid(logits)
            sfc = scores + gate_bias[None, :]
            grp = sfc.reshape(T, G, E // G)
            top2, _ = jax.lax.top_k(grp, 2)
            group_scores = top2.sum(-1)
            _, gidx = jax.lax.top_k(group_scores, TG)
            gmask = jnp.zeros((T, G), sfc.dtype).at[jnp.arange(T)[:, None], gidx].set(1.0)
            smask = jnp.repeat(gmask, E // G, axis=1) > 0
            tmp = jnp.where(smask, sfc, 0.0)
            _, topk_idx = jax.lax.top_k(tmp, K)
            topk_w = jnp.take_along_axis(scores, topk_idx, axis=1)
            topk_w = topk_w / (topk_w.sum(-1, keepdims=True) + 1e-20)
            return (topk_idx, topk_w * SCALE)
        key = jax.random.key(seed)
        ks = jax.random.split(key, 8)
        bound = 1.0 / np.sqrt(H)
        return {'hidden_states': jax.random.normal(ks[0], (1, 128, H), jnp.float32), 'gate_w': jax.random.uniform(ks[1], (E, H), jnp.float32, -bound, bound), 'gate_bias': jnp.zeros((E,), jnp.float32), 'gate_proj': jax.random.normal(ks[2], (E, I, H), jnp.float32) * 0.02, 'up_proj': jax.random.normal(ks[3], (E, I, H), jnp.float32) * 0.02, 'down_proj': jax.random.normal(ks[4], (E, H, I), jnp.float32) * 0.02, 'shared_gate_w': jax.random.normal(ks[5], (I * NS, H), jnp.float32) * 0.02, 'shared_up_w': jax.random.normal(ks[6], (I * NS, H), jnp.float32) * 0.02, 'shared_down_w': jax.random.normal(ks[7], (H, I * NS), jnp.float32) * 0.02}
    _L1_ffn_in = _L1_ffn_setup()
    _d = {'L0_attn_x': _L0_attn_in['x'], 'L0_attn_bv_q': _L0_attn_in['bv_q'], 'L0_attn_bv_k': _L0_attn_in['bv_k'], 'L0_attn_bv_v': _L0_attn_in['bv_v'], 'L0_ffn_gw': _L0_ffn_in['gw'], 'L0_ffn_gb': _L0_ffn_in['gb'], 'L0_ffn_w1': _L0_ffn_in['w1'], 'L0_ffn_b1': _L0_ffn_in['b1'], 'L0_ffn_w3': _L0_ffn_in['w3'], 'L0_ffn_b3': _L0_ffn_in['b3'], 'L0_ffn_w2': _L0_ffn_in['w2'], 'L0_ffn_b2': _L0_ffn_in['b2'], 'L0_ffn_sw1': _L0_ffn_in['sw1'], 'L0_ffn_sb1': _L0_ffn_in['sb1'], 'L0_ffn_sw3': _L0_ffn_in['sw3'], 'L0_ffn_sb3': _L0_ffn_in['sb3'], 'L0_ffn_sw2': _L0_ffn_in['sw2'], 'L0_ffn_sb2': _L0_ffn_in['sb2'], 'L1_attn_pos_emb_k': _L1_attn_in['pos_emb_k'], 'L1_attn_Wq': _L1_attn_in['Wq'], 'L1_attn_Wk': _L1_attn_in['Wk'], 'L1_attn_Wv': _L1_attn_in['Wv'], 'L1_attn_Wproj': _L1_attn_in['Wproj'], 'L1_ffn_gate_w': _L1_ffn_in['gate_w'], 'L1_ffn_gate_bias': _L1_ffn_in['gate_bias'], 'L1_ffn_gate_proj': _L1_ffn_in['gate_proj'], 'L1_ffn_up_proj': _L1_ffn_in['up_proj'], 'L1_ffn_down_proj': _L1_ffn_in['down_proj'], 'L1_ffn_shared_gate_w': _L1_ffn_in['shared_gate_w'], 'L1_ffn_shared_up_w': _L1_ffn_in['shared_up_w'], 'L1_ffn_shared_down_w': _L1_ffn_in['shared_down_w']}
    _x0 = _d['L0_attn_x']
    _d['L0_attn_x'] = jax.random.normal(jax.random.fold_in(jax.random.key(seed), 1), (2, 1024, 128), dtype=_x0.dtype)
    del _x0
    return _d

def reference(L0_attn_x, L0_attn_bv_q, L0_attn_bv_k, L0_attn_bv_v, L0_ffn_gw, L0_ffn_gb, L0_ffn_w1, L0_ffn_b1, L0_ffn_w3, L0_ffn_b3, L0_ffn_w2, L0_ffn_b2, L0_ffn_sw1, L0_ffn_sb1, L0_ffn_sw3, L0_ffn_sb3, L0_ffn_sw2, L0_ffn_sb2, L1_attn_pos_emb_k, L1_attn_Wq, L1_attn_Wk, L1_attn_Wv, L1_attn_Wproj, L1_ffn_gate_w, L1_ffn_gate_bias, L1_ffn_gate_proj, L1_ffn_up_proj, L1_ffn_down_proj, L1_ffn_shared_gate_w, L1_ffn_shared_up_w, L1_ffn_shared_down_w):

    def _L0_attn_ref(x, bv_q, bv_k, bv_v):
        import jax, jax.numpy as jnp
        import numpy as np
        DIM = 128
        N_HEADS = 16
        HEAD_DIM = DIM // N_HEADS
        SCALE = HEAD_DIM ** (-0.5)
        B, T, D = x.shape
        H, HD = (N_HEADS, HEAD_DIM)
        x_h = x.reshape(B, T, H, HD)
        Q = x_h * jnp.sign(bv_q)
        K = x_h * jnp.sign(bv_k)
        V = x_h * jnp.sign(bv_v)
        scores = jnp.einsum('bqhd,bkhd->bhqk', Q, K) * SCALE
        causal = jnp.tril(jnp.ones((T, T), dtype=bool))
        attn = jnp.where(causal, jax.nn.sigmoid(scores * 4.0), 0.0)
        out = jnp.einsum('bhqk,bkhd->bqhd', attn, V)
        return out.reshape(B, T, D)

    def _L0_ffn_ref(x, gw, gb, w1, b1, w3, b3, w2, b2, sw1, sb1, sw3, sb3, sw2, sb2):
        import jax, jax.numpy as jnp
        import numpy as np
        DIM = 128
        INTER = 64
        E = 32
        TOPK = 4
        GROUPS = 8
        TOPK_GROUPS = 4
        SHARED_INTER = 2 * INTER
        ROUTE_SCALE = 1.0
        B, S = (8, 512)

        def _gate(xf, gw, gb):
            T = xf.shape[0]
            scores = jax.nn.softmax((xf @ gw + gb).astype(jnp.float32), axis=-1)
            original_scores = scores
            scores_g = scores.reshape(T, GROUPS, E // GROUPS)
            group_scores = jnp.sum(jax.lax.top_k(scores_g, 2)[0], axis=-1)
            gidx = jax.lax.top_k(group_scores, TOPK_GROUPS)[1]
            keep = jnp.zeros((T, GROUPS), bool).at[jnp.arange(T)[:, None], gidx].set(True)
            masked = jnp.where(keep[:, :, None], scores_g, -jnp.inf).reshape(T, E)
            indices = jax.lax.top_k(masked, TOPK)[1]
            weights = jnp.take_along_axis(original_scores, indices, axis=1) * ROUTE_SCALE
            return (weights.astype(xf.dtype), indices)
        shape = x.shape
        xf = x.reshape(-1, DIM)
        T = xf.shape[0]
        weights, indices = _gate(xf, gw, gb)
        cw = jnp.zeros((T, E), xf.dtype).at[jnp.arange(T)[:, None], indices].add(weights)

        def body(y, p):
            w1e, b1e, w3e, b3e, w2e, b2e, we = p
            h = jax.nn.silu(xf @ w1e + b1e) * (xf @ w3e + b3e)
            return (y + we[:, None] * (h @ w2e + b2e), None)
        y0 = jnp.zeros_like(xf)
        y, _ = jax.lax.scan(body, y0, (w1, b1, w3, b3, w2, b2, cw.T))
        z = jax.nn.silu(xf @ sw1 + sb1) * (xf @ sw3 + sb3) @ sw2 + sb2
        return (y + z).reshape(shape)

    def _L1_attn_ref(x, pos_emb_k, Wq, Wk, Wv, Wproj):
        import jax, jax.numpy as jnp
        import numpy as np
        N_HEAD = 16
        POS_EMB_RADIUS = 128
        EMB = 128
        B, S, E = x.shape
        H = N_HEAD
        hd = E // H
        r = POS_EMB_RADIUS
        P = 2 * r
        q = (x @ Wq.T).reshape(B, S, H, hd).transpose(0, 2, 1, 3)
        k = (x @ Wk.T).reshape(B, S, H, hd).transpose(0, 2, 1, 3)
        v = (x @ Wv.T).reshape(B, S, H, hd).transpose(0, 2, 1, 3)
        att_rel_pos = jnp.einsum('bhsd,pd->bhsp', q, pos_emb_k)
        ar = jnp.arange(S)
        att_idxs = jnp.clip(ar[None, :] - ar[:, None], -r, r - 1) % P
        att_pos = att_rel_pos[:, :, ar[:, None], att_idxs]
        attn_val = jnp.einsum('bhqd,bhkd->bhqk', q, k)
        attn_scale = 1.0 / jnp.sqrt(jnp.asarray(hd, x.dtype))
        att = jax.nn.softmax((attn_val + att_pos) * attn_scale, axis=-1)
        y = jnp.einsum('bhqk,bhkd->bhqd', att, v)
        y = y.transpose(0, 2, 1, 3).reshape(B, S, E)
        return y @ Wproj.T

    def _L1_ffn_ref(hidden_states, gate_w, gate_bias, gate_proj, up_proj, down_proj, shared_gate_w, shared_up_w, shared_down_w):
        import jax, jax.numpy as jnp
        import numpy as np
        E = 16
        K = 4
        G = 4
        TG = 2
        NS = 2
        H = 128
        I = 176
        SCALE = 1.0

        def _gate(x2d, gate_w, gate_bias):
            T = x2d.shape[0]
            logits = x2d.astype(jnp.float32) @ gate_w.astype(jnp.float32).T
            scores = jax.nn.sigmoid(logits)
            sfc = scores + gate_bias[None, :]
            grp = sfc.reshape(T, G, E // G)
            top2, _ = jax.lax.top_k(grp, 2)
            group_scores = top2.sum(-1)
            _, gidx = jax.lax.top_k(group_scores, TG)
            gmask = jnp.zeros((T, G), sfc.dtype).at[jnp.arange(T)[:, None], gidx].set(1.0)
            smask = jnp.repeat(gmask, E // G, axis=1) > 0
            tmp = jnp.where(smask, sfc, 0.0)
            _, topk_idx = jax.lax.top_k(tmp, K)
            topk_w = jnp.take_along_axis(scores, topk_idx, axis=1)
            topk_w = topk_w / (topk_w.sum(-1, keepdims=True) + 1e-20)
            return (topk_idx, topk_w * SCALE)
        orig_shape = hidden_states.shape
        x = hidden_states.reshape(-1, H)
        topk_idx, topk_w = _gate(x, gate_w, gate_bias)
        combine_w = (jax.nn.one_hot(topk_idx, E, dtype=x.dtype) * topk_w[..., None]).sum(1)
        g = jnp.einsum('th,eih->tei', x, gate_proj)
        u = jnp.einsum('th,eih->tei', x, up_proj)
        act = jax.nn.silu(g) * u
        y = jnp.einsum('tei,ehi,te->th', act, down_proj, combine_w)
        sg = x @ shared_gate_w.T
        su = x @ shared_up_w.T
        y = y + jax.nn.silu(sg) * su @ shared_down_w.T
        return y.reshape(orig_shape)
    x = L0_attn_x
    xn = _layernorm(x, axis=-1)
    x = x + _L0_attn_ref(xn, L0_attn_bv_q, L0_attn_bv_k, L0_attn_bv_v) + _L0_ffn_ref(xn, L0_ffn_gw, L0_ffn_gb, L0_ffn_w1, L0_ffn_b1, L0_ffn_w3, L0_ffn_b3, L0_ffn_w2, L0_ffn_b2, L0_ffn_sw1, L0_ffn_sb1, L0_ffn_sw3, L0_ffn_sb3, L0_ffn_sw2, L0_ffn_sb2)
    xn = _layernorm(x, axis=-1)
    x = x + _L1_attn_ref(xn, L1_attn_pos_emb_k, L1_attn_Wq, L1_attn_Wk, L1_attn_Wv, L1_attn_Wproj) + _L1_ffn_ref(xn, L1_ffn_gate_w, L1_ffn_gate_bias, L1_ffn_gate_proj, L1_ffn_up_proj, L1_ffn_down_proj, L1_ffn_shared_gate_w, L1_ffn_shared_up_w, L1_ffn_shared_down_w)
    return x

_drawn_inputs = setup_inputs


def setup_inputs(seed=0):
    import zlib

    import numpy as np

    out = dict(_drawn_inputs(seed))
    spreads = {'L0_ffn_gb': (0.0, 0.8),
     'L0_ffn_b1': (0.0, 0.8),
     'L0_ffn_b3': (0.0, 0.8),
     'L0_ffn_b2': (0.0, 2.0),
     'L0_ffn_sb1': (0.0, 0.8),
     'L0_ffn_sb3': (0.0, 0.8),
     'L0_ffn_sb2': (0.0, 2.0),
     'L1_ffn_gate_bias': (0.0, 2.0)}
    factors = {'L0_ffn_gw': 8.0,
     'L0_ffn_w1': 8.0,
     'L0_ffn_w3': 8.0,
     'L0_ffn_w2': 8.0,
     'L0_ffn_sw1': 7.694,
     'L0_ffn_sw3': 7.25,
     'L0_ffn_sw2': 7.191,
     'L1_attn_pos_emb_k': 166.699,
     'L1_attn_Wq': 8.0,
     'L1_attn_Wk': 8.0,
     'L1_attn_Wv': 8.0,
     'L1_attn_Wproj': 8.0,
     'L1_ffn_gate_w': 64.0,
     'L1_ffn_gate_proj': 64.0,
     'L1_ffn_up_proj': 64.0,
     'L1_ffn_down_proj': 64.0,
     'L1_ffn_shared_gate_w': 36.647,
     'L1_ffn_shared_up_w': 32.846,
     'L1_ffn_shared_down_w': 32.949}
    for name, (base, spread) in spreads.items():
        noise = np.random.default_rng([zlib.crc32(name.encode()), seed]).standard_normal(out[name].shape)
        drawn = base * np.exp(spread * noise) if base else spread * noise
        out[name] = jnp.asarray(drawn.astype(out[name].dtype))
    for name, factor in factors.items():
        out[name] = (out[name] * factor).astype(out[name].dtype)
    return out
```

```python
from contextlib import ExitStack

import concourse.bass as bass
from concourse import mybir

F32 = mybir.dt.float32
F32R = mybir.dt.float32r
BF16 = mybir.dt.bfloat16
U32 = mybir.dt.uint32
ALU = mybir.AluOpType
ACT = mybir.ActivationFunctionType
AX = mybir.AxisListType

P = 128
B, T, D = 2, 1024, 128
N = B * T
NT = N // P
H, HD = 16, 8
NB = T // P
CH = 512
NC = N // CH
EPS = 1e-5
TERMS = 3
RADIUS = 128
BAND = 3 * P
RELROW = 4 * P

C_ID, C_CAUSAL, C_IOTA, C_TRI8, C_TRI4, C_POW = 0, 128, 256, 288, 352, 368
C_ALL = 384


class Layer:

    def __init__(self, index, experts, group, top_groups, rows):
        self.index, self.E, self.per_group, self.top_groups = index, experts, group, top_groups
        self.G = experts // group
        self.rows = rows
        self.chunks = [min(P, rows - c) for c in range(0, rows, P)]


L0 = Layer(0, 32, 4, 4, 32 * 64 + 128)
L1 = Layer(1, 16, 4, 2, 16 * 176 + 352)
TOP = 4
LO_ROW = 64


def view(ap, *free):
    return bass.AP(ap.tensor, ap.offset, [ap.ap[0], *[list(f) for f in free]])


def f32(ap):
    return ap.bitcast(F32)


def flat(t):
    ap = t[:]
    return ap if len(ap.shape) == 2 else ap.rearrange("p a b -> p (a b)")


def prepare(nc, d, sb, scr, layer):
    k = layer.index
    with ExitStack() as ctx:
        def tile(name, shape, dt=F32):
            return ctx.enter_context(nc.sbuf_tensor(f"{name}_{k}", shape, dt))

        def sem(name):
            return ctx.enter_context(nc.semaphore(f"{name}_{k}"))

        E, G, PG = layer.E, layer.G, layer.per_group
        sq = tile("sq", [P, NT, D])
        stat = tile("stat", [P, 4, NT])
        gw = tile("gw", [P, E]); gw_hi = tile("gw_hi", [P, E], F32R); gw_lo = tile("gw_lo", [P, E], F32R)
        gb = tile("gb", [P, E])
        sc = tile("sc", [P, NT, E]); biased = tile("biased", [P, NT, E]); masked = tile("masked", [P, NT, E])
        pair = tile("pair", [P, 6, NT * G]); gs = tile("gs", [P, NT, G])
        cmp_a = tile("cmp_a", [P, NT, G * G]); cmp_b = tile("cmp_b", [P, NT, G * G])
        keep = tile("keep", [P, NT, G]); keep1 = tile("keep1", [P, NT, G])
        top = tile("top", [P, NT, 8]); topi = tile("topi", [P, NT, 8], U32); topf = tile("topf", [P, NT, 8])
        hot = tile("hot", [P, 2, NT, E]); cw = tile("cw", [P, NT, E + 1])
        rs = tile("rs", [P, 2, NT])
        bank = [ctx.enter_context(nc.psum_tensor(f"bank{i}_{k}", [P, CH], F32)) for i in range(8)]
        if k == 0:
            sgn = tile("sgn", [P, 2, 4]); sgv = tile("sgv", [P, 2, D])
            q_hi = tile("q_hi", [P, N], F32R); q_lo = tile("q_lo", [P, N], F32R)
        else:
            wqkv = tile("wqkv", [P, 3, D]); w_hi = tile("w_hi", [P, 3, D], F32R); w_lo = tile("w_lo", [P, 3, D], F32R)
            ecol = tile("ecol", [P, 2])
            q_hi = tile("q_hi", [P, N], F32R); q_lo = tile("q_lo", [P, N], F32R)
            k_hi = [tile(f"k_hi{v}", [P, N], F32R) for v in range(2)]
            k_lo = [tile(f"k_lo{v}", [P, N], F32R) for v in range(2)]

        loaded, x_loaded = sem("loaded"), sem("x_loaded")
        mean_done, var_ready, rstd_ready, xn_ready = sem("mean_done"), sem("var_ready"), sem("rstd_ready"), sem("xn_ready")
        turned, hi_ready, lo_ready = sem("turned"), sem("hi_ready"), sem("lo_ready")
        gw_ready, logits_ready, exp_in, exp_ready = sem("gw_ready"), sem("logits_ready"), sem("exp_in"), sem("exp_ready")
        cw_ready, cw_turned, cw_hi_done, cw_done = sem("cw_ready"), sem("cw_turned"), sem("cw_hi_done"), sem("cw_done")
        step, stored, att_ready = sem("step"), sem("stored"), sem("att_ready")
        back, x_ready, w_ready, proj_ready, proj_hi, proj_used = (sem("back"), sem("x_ready"), sem("w_ready"),
                                                        sem("proj_ready"), sem("proj_hi"), sem("proj_used"))
        ident = sb["const"][:, C_ID:C_ID + P]
        xn, x_hi, x_lo = sb["xn"], sb["x_hi"], sb["x_lo"]
        block = ctx.enter_context(nc.Block())

        @block.sync
        def _(sp):
            if k == 0:
                sp.dma_start(sb["x"][:], d["x"].rearrange("(t p) d -> p t d", p=P)).then_inc(x_loaded, 16)
                sp.dma_start(sb["const"][:], d["const"]).then_inc(x_loaded, 16)
                sp.dma_start(gw[:], d["gw0"]).then_inc(loaded, 16)
                sp.dma_start(gb[:], d["gb0"].partition_broadcast(P)).then_inc(loaded, 16)
                sp.dma_start(sgn[:, 0, 0:2], d["bqk"]).then_inc(loaded, 16)
                sp.dma_start(sgv[:, 0, :], d["bv"].partition_broadcast(P)).then_inc(loaded, 16)
                for w, (src, ready, n) in enumerate(((x_hi, hi_ready, NC), (x_hi, hi_ready, NC), (x_lo, lo_ready, NC))):
                    sp.wait_ge(ready, n)
                    sp.dma_start(scr["k0"][w], f32(src[:]).rearrange("p (b t) -> p b t", b=B)).then_inc(stored, 16)
                for w, src in enumerate((q_hi, q_lo, q_hi)):
                    sp.wait_ge(att_ready, 2)
                    sp.dma_start(scr["q0"][w], f32(src[:]).rearrange("p (b t) -> p b t", b=B)).then_inc(stored, 16)
                sp.wait_ge(stored, 16 * 6)
            else:
                sp.dma_start(gw[:], d["gw1"]).then_inc(loaded, 16)
                sp.dma_start(gb[:], d["gb1"].partition_broadcast(P)).then_inc(loaded, 16)
                sp.dma_start(wqkv[:], d["wqkv"]).then_inc(loaded, 16)
                sp.dma_start(ecol[:], d["ecol"]).then_inc(loaded, 16)
                n = 0
                for name, hi, lo, order in (("q1", q_hi, q_lo, "hlh"), ("ka", k_hi[0], k_lo[0], "hhl"),
                                            ("kb", k_hi[1], k_lo[1], "hhl")):
                    sp.wait_ge(proj_used, NC if name == "q1" else 2 * NC)
                    for w, part in enumerate(order):
                        src = hi if part == "h" else lo
                        sp.dma_start(scr[name][w], f32(src[:]).rearrange("p (b t) -> p b t", b=B)).then_inc(stored, 16)
                        n += 1
                sp.wait_ge(stored, 16 * n)

        @block.tensor
        def _(pe):
            if k == 1:
                for t in range(NT):
                    ins = pe.transpose(bank[t // 4][:, (t % 4) * P:(t % 4 + 1) * P], sb["yT"][:, t * P:(t + 1) * P], ident)
                    if t % 4 == 3:
                        ins.then_inc(back, 1)
                pe.wait_ge(x_ready, NC)
            pe.wait_ge(x_loaded, 32) if k == 0 else None
            pe.wait_ge(xn_ready, 1)
            for t in range(NT):
                ins = pe.transpose(bank[t // 4][:, (t % 4) * P:(t % 4 + 1) * P], xn[:, t, :], ident)
                if t % 4 == 3:
                    ins.then_inc(turned, 1)
            pe.wait_ge(gw_ready, 2)
            for t in range(NT):
                if t % 4 == 0:
                    pe.wait_ge(lo_ready, t // 4 + 1)
                    pe.wait_ge(hi_ready, t // 4 + 1)
                cols = slice(t * P, (t + 1) * P)
                out = bank[4][:, t * E:(t + 1) * E]
                pe.matmul(out, x_hi[:, cols], gw_hi[:], start=True, stop=False)
                pe.matmul(out, x_lo[:, cols], gw_hi[:], start=False, stop=False)
                ins = pe.matmul(out, x_hi[:, cols], gw_lo[:], start=False, stop=True)
            ins.then_inc(logits_ready, 1)
            if k == 1:
                pe.wait_ge(w_ready, 2)
                n = 0
                for w in range(2):
                    for c in range(NC):
                        if n >= 2:
                            pe.wait_ge(proj_used, n - 1)
                        out, cols = bank[5 + n % 2][:], slice(c * CH, (c + 1) * CH)
                        pe.matmul(out, w_hi[:, w, :], x_hi[:, cols], start=True, stop=False)
                        pe.matmul(out, w_lo[:, w, :], x_hi[:, cols], start=False, stop=False)
                        pe.matmul(out, w_hi[:, w, :], x_lo[:, cols], start=False, stop=True).then_inc(proj_ready, 1)
                        n += 1
                for t in range(NT):
                    if t % 4 == 0 and t >= 4:
                        pe.wait_ge(proj_used, 2 * NC + t // 4 - 1 if t >= 8 else 2 * NC)
                    out, cols = bank[(7, 5)[t // 4 % 2]][:, (t % 4) * P:(t % 4 + 1) * P], slice(t * P, (t + 1) * P)
                    pe.matmul(out, x_hi[:, cols], w_hi[:, 2, :], start=True, stop=False)
                    pe.matmul(out, x_lo[:, cols], w_hi[:, 2, :], start=False, stop=False)
                    ins = pe.matmul(out, x_hi[:, cols], w_lo[:, 2, :], start=False, stop=True)
                    if t % 4 == 3:
                        ins.then_inc(proj_ready, 1)
            pe.wait_ge(cw_ready, 1)
            pe.wait_ge(lo_ready, NC)
            for t in range(NT):
                ins = pe.transpose(bank[t // 4][0:E + 1, (t % 4) * P:(t % 4 + 1) * P], cw[:, t, :], ident)
                if t % 4 == 3:
                    ins.then_inc(cw_turned, 1)

        @block.scalar
        def _(act):
            for c in range(NC):
                act.wait_ge(turned, c + 1)
                act.activation(x_hi[:, c * CH:(c + 1) * CH], bank[c][:], ACT.Copy).then_inc(hi_ready, 1)
            act.wait_ge(exp_in, 1)
            act.activation(sc[:], sc[:], ACT.Exp if k == 0 else ACT.Sigmoid).then_inc(exp_ready, 1)
            if k == 1:
                for c in range(NC):
                    act.wait_ge(proj_ready, c + 1)
                    act.activation(q_hi[:, c * CH:(c + 1) * CH], bank[5 + c % 2][:], ACT.Copy).then_inc(proj_hi, 1)
            for c in range(NC):
                act.wait_ge(cw_turned, c + 1)
                if c == 0:
                    act.wait_ge(cw_done, 1)
                act.activation(sb["cw_split"][0:E + 1, c * CH:(c + 1) * CH], bank[c][0:E + 1, :], ACT.Copy).then_inc(cw_hi_done, 1)

        @block.gpsimd
        def _(pool):
            pool.memset(f32(sb["cw_split"][:]), 0.0).then_inc(cw_done, 1)
            pool.memset(cw[:, :, E:E + 1], 1.0).then_inc(cw_done, 1)
            if k == 0:
                pool.wait_ge(x_loaded, 32)
            pool.wait_ge(var_ready, 1)
            pool.tensor_tensor(stat[:, 3, :], stat[:, 2, :], sb["const"][:, C_POW:C_POW + NT], ALU.pow).then_inc(rstd_ready, 1)

        @block.vector
        def _(dve):
            count = [0]

            def then(ins):
                count[0] += 1
                ins.then_inc(step, 1)
                dve.wait_ge(step, count[0])

            def per_tile(ap):
                return view(ap, [1, NT], [0, D])

            x = sb["x"]
            if k == 0:
                dve.wait_ge(x_loaded, 32)
            else:
                for c in range(NC):
                    dve.wait_ge(back, c + 1)
                    part = x[:, 4 * c:4 * c + 4, :]
                    dve.tensor_tensor(part, bank[c][:].rearrange("p (t d) -> p t d", d=D), part, ALU.add).then_inc(x_ready, 1)
                dve.wait_ge(x_ready, NC)
            then(dve.tensor_reduce(stat[:, 0, :], x[:], AX.X, ALU.add))
            then(dve.tensor_scalar(stat[:, 1, :], stat[:, 0, :], 1.0 / D, None, ALU.mult))
            then(dve.tensor_tensor(xn[:], x[:], per_tile(stat[:, 1, :]), ALU.subtract))
            then(dve.tensor_tensor(sq[:], xn[:], xn[:], ALU.mult))
            then(dve.tensor_reduce(stat[:, 0, :], sq[:], AX.X, ALU.add))
            dve.tensor_scalar(stat[:, 2, :], stat[:, 0, :], 1.0 / D, EPS, ALU.mult, ALU.add).then_inc(var_ready, 1)
            dve.wait_ge(loaded, 64)
            then(dve.tensor_copy(gw_hi[:], gw[:]))
            dve.tensor_tensor(gw_lo[:], gw[:], f32(gw_hi[:]), ALU.subtract).then_inc(gw_ready, 2)
            dve.wait_ge(rstd_ready, 1)
            dve.tensor_tensor(xn[:], xn[:], per_tile(stat[:, 3, :]), ALU.mult).then_inc(xn_ready, 1)
            if k == 0:
                then(dve.tensor_scalar(sgn[:, 1, 0:2], sgn[:, 0, 0:2], 0.0, None, ALU.is_gt))
                then(dve.tensor_scalar(sgn[:, 1, 2:4], sgn[:, 0, 0:2], 0.0, None, ALU.is_lt))
                then(dve.tensor_tensor(sgn[:, 0, 0:2], sgn[:, 1, 0:2], sgn[:, 1, 2:4], ALU.subtract))
                then(dve.tensor_tensor(sgn[:, 0, 2:3], sgn[:, 0, 0:1], sgn[:, 0, 1:2], ALU.mult))
                then(dve.tensor_scalar(sgv[:, 1, :], sgv[:, 0, :], 0.0, None, ALU.is_gt))
                then(dve.tensor_scalar(sgv[:, 0, :], sgv[:, 0, :], 0.0, None, ALU.is_lt))
                then(dve.tensor_tensor(sgv[:, 1, :], sgv[:, 1, :], sgv[:, 0, :], ALU.subtract))
                dve.wait_ge(xn_ready, 1)
                for b in range(B):
                    out = view(sb["v"][:, b * NB * D:], [HD, NB], [NB * HD, H], [1, HD])
                    src = view(xn[:, b * NB, :], [D, NB], [HD, H], [1, HD])
                    dve.tensor_tensor(out, src, view(sgv[:, 1, :], [0, NB], [HD, H], [1, HD]), ALU.mult)
            else:
                then(dve.tensor_copy(w_hi[:], wqkv[:]))
                dve.tensor_tensor(w_lo[:], wqkv[:], f32(w_hi[:]), ALU.subtract).then_inc(w_ready, 2)
            for c in range(NC):
                cols = slice(c * CH, (c + 1) * CH)
                dve.wait_ge(hi_ready, c + 1)
                dve.tensor_tensor(x_lo[:, cols], bank[c][:], f32(x_hi[:, cols]), ALU.subtract).then_inc(lo_ready, 1)
            if k == 0:
                dve.wait_ge(lo_ready, NC)
                dve.tensor_scalar(q_hi[:], f32(x_hi[:]), sgn[:, 0, 2:3], None, ALU.mult).then_inc(att_ready, 1)
                dve.tensor_scalar(q_lo[:], f32(x_lo[:]), sgn[:, 0, 2:3], None, ALU.mult).then_inc(att_ready, 1)
            dve.wait_ge(logits_ready, 1)
            logits = bank[4][:, 0:NT * E].rearrange("p (t e) -> p t e", e=E)
            if k == 0:
                then(dve.tensor_tensor(sc[:], logits, view(gb[:], [0, NT], [1, E]), ALU.add))
                then(dve.tensor_reduce(rs[:, 0, :], sc[:], AX.X, ALU.max))
                dve.tensor_tensor(sc[:], sc[:], view(rs[:, 0, :], [1, NT], [0, E]), ALU.subtract).then_inc(exp_in, 1)
                dve.wait_ge(exp_ready, 1)
                then(dve.tensor_reduce(rs[:, 0, :], sc[:], AX.X, ALU.add))
                then(dve.reciprocal(rs[:, 1, :], rs[:, 0, :]))
                then(dve.tensor_tensor(sc[:], sc[:], view(rs[:, 1, :], [1, NT], [0, E]), ALU.mult))
                chosen = sc
            else:
                dve.tensor_copy(sc[:], logits).then_inc(exp_in, 1)
                for c in range(NC):
                    cols = slice(c * CH, (c + 1) * CH)
                    dve.wait_ge(proj_hi, c + 1)
                    dve.tensor_tensor(q_lo[:, cols], bank[5 + c % 2][:], f32(q_hi[:, cols]), ALU.subtract).then_inc(proj_used, 1)
                for c in range(NC):
                    cols = slice(c * CH, (c + 1) * CH)
                    src = bank[5 + (NC + c) % 2][:]
                    dve.wait_ge(proj_ready, NC + c + 1)
                    for v in range(2):
                        then(dve.tensor_scalar(k_hi[v][:, cols], src, ecol[:, v:v + 1], None, ALU.add))
                    for v in range(2):
                        ins = dve.scalar_tensor_tensor(k_lo[v][:, cols], src, ecol[:, v:v + 1], f32(k_hi[v][:, cols]), ALU.add, ALU.subtract)
                    ins.then_inc(proj_used, 1)
                for c in range(NC):
                    dve.wait_ge(proj_ready, 2 * NC + c + 1)
                    b, j0 = c // 2, 4 * (c % 2)
                    out = view(sb["v"][:, b * NB * D + j0 * HD:], [HD, 4], [NB * HD, H], [1, HD])
                    src = view(bank[(7, 5)[c % 2]][:], [D, 4], [HD, H], [1, HD])
                    dve.tensor_copy(out, src).then_inc(proj_used, 1)
                dve.wait_ge(exp_ready, 1)
                then(dve.tensor_tensor(biased[:], sc[:], view(gb[:], [0, NT], [1, E]), ALU.add))
                chosen = biased
            quad = chosen[:].rearrange("p t (g e) -> p (t g) e", e=PG)
            hi1, lo1, hi2, lo2, mx, mn = (pair[:, i, :] for i in range(6))
            dve.tensor_tensor(hi1, quad[:, :, 0], quad[:, :, 1], ALU.max)
            dve.tensor_tensor(lo1, quad[:, :, 0], quad[:, :, 1], ALU.min)
            dve.tensor_tensor(hi2, quad[:, :, 2], quad[:, :, 3], ALU.max)
            then(dve.tensor_tensor(lo2, quad[:, :, 2], quad[:, :, 3], ALU.min))
            dve.tensor_tensor(mx, hi1, hi2, ALU.max)
            then(dve.tensor_tensor(mn, hi1, hi2, ALU.min))
            then(dve.tensor_tensor(lo1, lo1, lo2, ALU.max))
            then(dve.tensor_tensor(mn, mn, lo1, ALU.max))
            then(dve.tensor_tensor(gs[:].rearrange("p t g -> p (t g)"), mx, mn, ALU.add))
            one, other = view(gs[:], [G, NT], [1, G], [0, G]), view(gs[:], [G, NT], [0, G], [1, G])
            square = [[G * G, NT], [G, G], [1, G]]
            tri = sb["const"][:, (C_TRI8 if G == 8 else C_TRI4):]
            then(dve.tensor_tensor(view(cmp_a[:], *square), other, one, ALU.is_equal))
            then(dve.tensor_tensor(cmp_a[:], cmp_a[:], view(tri, [0, NT], [1, G * G]), ALU.mult))
            then(dve.tensor_tensor(view(cmp_b[:], *square), other, one, ALU.is_gt))
            then(dve.tensor_tensor(cmp_a[:], cmp_a[:], cmp_b[:], ALU.add))
            then(dve.tensor_reduce(keep[:], view(cmp_a[:], *square), AX.X, ALU.add))
            then(dve.tensor_scalar(keep[:], keep[:], float(layer.top_groups), None, ALU.is_lt))
            kept = view(keep[:], [G, NT], [1, G], [0, PG])
            by_group = [[E, NT], [PG, G], [1, PG]]
            then(dve.tensor_tensor(view(masked[:], *by_group), view(chosen[:], *by_group), kept, ALU.mult))
            if k == 0:
                then(dve.tensor_scalar(keep1[:], keep[:], 1.0, None, ALU.subtract))
                then(dve.tensor_tensor(view(masked[:], *by_group), view(masked[:], *by_group),
                                       view(keep1[:], [G, NT], [1, G], [0, PG]), ALU.add))
            else:
                then(dve.tensor_scalar(masked[:], masked[:], 0.0, None, ALU.add))
            for t in range(NT):
                ins = dve.max(top[:, t, :], masked[:, t, :])
            then(ins)
            for t in range(NT):
                ins = dve.max_index(topi[:, t, :], top[:, t, :], masked[:, t, :])
            then(ins)
            then(dve.tensor_copy(topf[:], topi[:]))
            iota = view(sb["const"][:, C_IOTA:], [0, NT], [1, E])
            for i in range(TOP):
                then(dve.tensor_tensor(hot[:, min(i, 1)], iota, view(topf[:, 0, i:], [8, NT], [0, E]), ALU.is_equal))
                if i:
                    then(dve.tensor_tensor(hot[:, 0], hot[:, 0], hot[:, 1], ALU.add))
            dve.wait_ge(cw_done, 2)
            if k == 0:
                dve.tensor_tensor(cw[:, :, 0:E], hot[:, 0], sc[:], ALU.mult).then_inc(cw_ready, 1)
            else:
                then(dve.tensor_tensor(hot[:, 0], hot[:, 0], sc[:], ALU.mult))
                then(dve.tensor_reduce(rs[:, 0, :], hot[:, 0], AX.X, ALU.add))
                then(dve.tensor_scalar(rs[:, 0, :], rs[:, 0, :], 1e-20, None, ALU.add))
                then(dve.reciprocal(rs[:, 1, :], rs[:, 0, :]))
                dve.tensor_tensor(cw[:, :, 0:E], hot[:, 0], view(rs[:, 1, :], [1, NT], [0, E]), ALU.mult).then_inc(cw_ready, 1)
            for c in range(NC):
                cols = slice(c * CH, (c + 1) * CH)
                dve.wait_ge(cw_hi_done, c + 1)
                dve.tensor_tensor(sb["cw_split"][LO_ROW:LO_ROW + E + 1, cols], bank[c][0:E + 1, :],
                                  f32(sb["cw_split"][0:E + 1, cols]), ALU.subtract).then_inc(cw_done, 1)


def sigmoid_attention(nc, d, sb, scr):
    SCALE = 4.0 * HD ** -0.5
    HALF, QUARTER = T // 2, T // 4
    PAIRS = B * H // 2
    with ExitStack() as ctx:
        def tile(name, shape, dt=F32):
            return ctx.enter_context(nc.sbuf_tensor("a0_" + name, shape, dt))

        def sem(name):
            return ctx.enter_context(nc.semaphore("a0_" + name))

        qs = tile("q", [P, 2, HALF], F32R)
        ks = tile("k", [P, 2, T], F32R)
        vs = tile("v", [P, 2, NB, 32])
        probs = tile("probs", [P, 4, T])
        ys = tile("y", [P, 2, QUARTER])
        st = [ctx.enter_context(nc.psum_tensor(f"a0_st{i}", [P, T], F32)) for i in range(2)]
        acc = [ctx.enter_context(nc.psum_tensor(f"a0_acc{i}", [P, CH], F32)) for i in range(2)]

        qk_loaded = [sem(f"qk_loaded{s}") for s in range(2)]
        y_stored = [sem(f"y_stored{s}") for s in range(2)]
        cleared, v_ready, st_ready, masked = sem("cleared"), sem("v_ready"), sem("st_ready"), sem("masked")
        passed = sem("passed")
        sig_done = sem("sig_done")
        probs_used = sem("probs_used")
        y_saved = sem("y_saved")
        block = ctx.enter_context(nc.Block())

        @block.sync
        def _(sp):
            def load(n, s):
                for g in range(2):
                    for w in range(TERMS):
                        rows = slice(64 * g + w * HD, 64 * g + (w + 1) * HD)
                        sp.dma_start(f32(qs[rows, s, :]), scr["q0h"][w, bass.ds(n, 1), :, g * HALF:(g + 1) * HALF]
                                     .rearrange("a r t -> (a r) t")).then_inc(qk_loaded[s], 16)
                        sp.dma_start(f32(ks[rows, s, :]), scr["k0h"][w, bass.ds(n, 1)]
                                     .rearrange("a r t -> (a r) t")).then_inc(qk_loaded[s], 16)

            def store(n, s):
                sp.wait_ge(y_saved, n + 3)
                sp.sem_inc(passed, 1)
                for r in range(4):
                    sp.dma_start(scr["y0h"][bass.ds(n, 1), :, r * QUARTER:(r + 1) * QUARTER].rearrange("a r t -> (a r) t"),
                                 ys[32 * r:32 * r + HD, s, :]).then_inc(y_stored[s], 16)

            for s in range(2):
                load(s, s)
            with sp.Fori(0, PAIRS - 1) as i:
                for s in range(2):
                    sp.wait_ge(probs_used, 16 * i + 8 * s + 8 + 4)
                    sp.sem_inc(passed, 1)
                    load(2 * i + s + 2, s)
                    store(2 * i + s, s)
            for s in range(2):
                store(2 * PAIRS - 2 + s, s)
            for s in range(2):
                sp.wait_ge(y_stored[s], 64 * PAIRS + 16)

        @block.gpsimd
        def _(pool):
            def copy_v(n, s):
                pool.tensor_copy(vs[:, s, :, 0:HD], sb["v"][:, bass.ds(n * (NB * HD), NB * HD)]
                                 .rearrange("p (j d) -> p j d", d=HD)).then_inc(v_ready, 1)

            pool.memset(vs[:], 0.0).then_inc(cleared, 1)
            pool.wait_ge(cleared, 1)
            for s in range(2):
                copy_v(s, s)
            with pool.Fori(0, PAIRS - 1) as i:
                for s in range(2):
                    pool.wait_ge(probs_used, 16 * i + 8 * s + 8 + 4)
                    copy_v(2 * i + s + 2, s)

        @block.tensor
        def _(pe):
            with pe.Fori(0, PAIRS) as i:
                def scores(s, j):
                    if j == 0:
                        pe.wait_ge(qk_loaded[s], 192 * i + 192)
                    pe.wait_ge(sig_done, 16 * i + 8 * s + j + 1)
                    for g in range(2):
                        lo = max(j * P - g * HALF, 0)
                        if lo < HALF:
                            rows = slice(64 * g, 64 * g + TERMS * HD)
                            ins = pe.matmul(st[j % 2][:, g * HALF + lo:(g + 1) * HALF], ks[rows, s, j * P:(j + 1) * P],
                                            qs[rows, s, lo:HALF], start=True, stop=True)
                    ins.then_inc(st_ready, 1)

                def values(s, j):
                    if j == 0:
                        pe.wait_ge(v_ready, 2 * i + s + 1)
                        pe.wait_ge(y_saved, 2 * i + s + 1)
                    pe.wait_ge(masked, 16 * i + 8 * s + j + 1)
                    for r in range(4):
                        lo = max(j * P - r * QUARTER, 0)
                        if lo < QUARTER:
                            ins = pe.matmul(acc[s][32 * r:32 * r + 32, lo:QUARTER], vs[:, s, j, :],
                                            probs[:, j % 4, r * QUARTER + lo:(r + 1) * QUARTER],
                                            start=(j == 0), stop=(j == 2 * r + 1))
                    ins.then_inc(probs_used, 1)

                for s in range(2):
                    for j in range(NB):
                        scores(s, j)
                        if j or s:
                            values(s if j else 0, (j - 1) % NB)
                values(1, NB - 1)

        @block.scalar
        def _(act):
            act.sem_inc(sig_done, 2)
            with act.Fori(0, PAIRS) as i:
                for s in range(2):
                    for j in range(NB):
                        act.wait_ge(st_ready, 16 * i + 8 * s + j + 1)
                        act.wait_ge(probs_used, 16 * i + 8 * s + j + 1)
                        act.activation(probs[:, j % 4, j * P:], st[j % 2][:, j * P:], ACT.Sigmoid, scale=SCALE).then_inc(sig_done, 1)

        @block.vector
        def _(dve):
            dve.sem_inc(y_saved, 2)
            dve.sem_inc(probs_used, 4)
            for s in range(2):
                dve.sem_inc(y_stored[s], 16)
            with dve.Fori(0, PAIRS) as i:
                for s in range(2):
                    for j in range(NB):
                        dve.wait_ge(sig_done, 16 * i + 8 * s + j + 3)
                        part = probs[:, j % 4, j * P:(j + 1) * P]
                        dve.tensor_tensor(part, part, sb["const"][:, C_CAUSAL:C_CAUSAL + P], ALU.mult).then_inc(masked, 1)
                    dve.wait_ge(probs_used, 16 * i + 8 * s + 8 + 4)
                    dve.wait_ge(y_stored[s], 64 * i + 16)
                    dve.tensor_copy(ys[:, s, :], acc[s][:, 0:QUARTER]).then_inc(y_saved, 1)


def softmax_attention(nc, d, sb, scr):
    SCALE = HD ** -0.5
    K3 = TERMS * HD
    MROW = 32
    LEAD = 6
    BLOCKS = B * H * NB
    RD = 16
    with ExitStack() as ctx:
        def tile(name, shape, dt=F32):
            return ctx.enter_context(nc.sbuf_tensor("a1_" + name, shape, dt))

        def sem(name):
            return ctx.enter_context(nc.semaphore("a1_" + name))

        qs = tile("q", [P, 2, T], F32R)
        ks = [tile(n, [P, 2, T // 2], F32R) for n in ("ka", "kb")]
        vs = tile("v", [P, 2, NB, 32])
        probs = tile("probs", [P, 8, T])
        rel_sb = tile("rel", [P, 4, BAND]); rel_raw = tile("rel_raw", [P, 4, BAND])
        rel_part = [tile(f"rel_part{n}", [P, 8, BAND], BF16) for n in range(3)]
        rel_rest = tile("rel_rest", [P, 4, BAND])
        negmax = tile("negmax", [P, 4]); ys = tile("y", [P, 2, P])
        ident_b = tile("ident_b", [P, P], BF16)
        emb = tile("emb", [K3, 3, BAND]); emb_hi = tile("emb_hi", [K3, BAND], F32R); emb_all = tile("emb_all", [K3, BAND], F32R)
        ecol = tile("ecol", [K3, 4]); zeros = tile("zeros", [P, P])
        s_ps = ctx.enter_context(nc.psum_tensor("a1_s_ps", [P, T], F32))
        rel_ps = ctx.enter_context(nc.psum_tensor("a1_rel_ps", [P, CH], F32))
        acc = ctx.enter_context(nc.psum_tensor("a1_acc_ps", [P, CH], F32))
        st = [ctx.enter_context(nc.psum_tensor(f"a1_st_ps{i}", [P, T], F32)) for i in range(2)]
        ident = sb["const"][:, C_ID:C_ID + P]
        max_row = rel_ps[0:1, BAND:BAND + P]

        loaded, cleared, step, emb_ready, zeroed = sem("loaded"), sem("cleared"), sem("step"), sem("emb_ready"), sem("zeroed")
        q_loaded = [sem(f"q_loaded{s}") for s in range(2)]
        k_loaded = [sem(f"k_loaded{s}") for s in range(2)]
        rel_written = [sem(f"rel_written{s}") for s in range(4)]
        rel_read = [sem(f"rel_read{s}") for s in range(4)]
        y_stored = [sem(f"y_stored{s}") for s in range(2)]
        rel_ready, rel_saved, hi_ready, lo_ready = sem("rel_ready"), sem("rel_saved"), sem("hi_ready"), sem("lo_ready")
        s_ready, max_ready, row_ready, row_saved = sem("s_ready"), sem("max_ready"), sem("row_ready"), sem("row_saved")
        st_ready, v_ready = sem("st_ready"), sem("v_ready")
        passed = sem("passed")
        rest_ready, mid_ready = sem("rest_ready"), sem("mid_ready")
        exp_done = sem("exp_done")
        pv_done = sem("pv_done")
        y_saved = sem("y_saved")

        def wait(eng, s, value):
            if not isinstance(value, int) or value > 0:
                eng.wait_ge(s, value)

        def pipeline(eng, one):
            for k in range(-LEAD, 4):
                one(0, k)
            with eng.Fori(0, BLOCKS // 16 - 1) as i:
                for k in range(4, 20):
                    one(i, k)
            for k in range(BLOCKS - 12, BLOCKS + 4):
                one(0, k)

        def there(k, lead=0):
            return 0 <= k + lead < BLOCKS

        def slot(k):
            return k // NB % 2

        block = ctx.enter_context(nc.Block())

        @block.sync
        def _(sp):
            sp.dma_start(emb[:, 0, :], d["emb"]).then_inc(loaded, 16)
            sp.dma_start(ecol[:], d["ecol24"]).then_inc(loaded, 16)
            sp.wait_ge(zeroed, 1)
            sp.dma_start(scr["rel"][:, :, 0:P - 1].rearrange("s p u -> p s u"), view(zeros[:], [0, RD], [1, P - 1])).then_inc(loaded, 16)
            sp.wait_ge(loaded, 48)
            sp.wait_ge(cleared, 4)

            def load(name, dst, n, s, loaded):
                for g in range(2):
                    src = scr[name][:, bass.ds(n, 1)]
                    if name != "q1h":
                        src = src[:, :, :, g * (T // 2):(g + 1) * (T // 2)]
                    sp.dma_start(f32(dst[64 * g:64 * g + K3, s, :]), src.rearrange("w a r t -> w (a r) t")).then_inc(loaded[s], 16)

            def one(i, k):
                if k == -LEAD:
                    load("q1h", qs, 0, 0, q_loaded)
                    load("kah", ks[0], 0, 0, k_loaded)
                    load("kbh", ks[1], 0, 0, k_loaded)
                if there(k, 5):
                    x = k + 5
                    sp.wait_ge(rel_written[x % 4], 64 * i + 16 * (x // 4) + 16)
                    sp.sem_inc(passed, 1)
                    wait(sp, lo_ready, 16 * i + x - 3)
                    sp.sem_inc(passed, 1)
                    row = scr["rel"][x % RD]
                    skewed = bass.AP(row.tensor, row.offset + P - 1, [[RELROW - 1, P], [1, BAND]])
                    sp.dma_start(rel_raw[:, x % 4, :], skewed).then_inc(rel_read[x % 4], 16)
                if there(k, 6):
                    x = k + 6
                    sp.wait_ge(rel_saved, 16 * i + x + 1)
                    sp.sem_inc(passed, 1)
                    sp.dma_start(scr["rel"][x % RD, :, P - 1:P - 1 + BAND], rel_sb[:, x % 4, :]).then_inc(rel_written[x % 4], 16)
                if k >= 0 and k - k % NB + NB < BLOCKS and k % NB < 3:
                    first = k - k % NB
                    if k == first:
                        wait(sp, st_ready, 16 * i + k)
                        sp.sem_inc(passed, 1)
                    name, dst, loaded_ = (("q1h", qs, q_loaded), ("kah", ks[0], k_loaded), ("kbh", ks[1], k_loaded))[k % NB]
                    load(name, dst, 2 * i + k // NB + 1, slot(k + NB), loaded_)
                if k >= 4 and k % 4 == 3:
                    batch = k // 4 - 1
                    sp.wait_ge(y_saved, 4 * i + batch + 2)
                    sp.sem_inc(passed, 1)
                    for q in range(4):
                        tile_i = batch % 2 * 4 + q
                        sp.dma_start(scr["y1s"][bass.ds(2 * i + batch // 2, 1), :, tile_i * P:(tile_i + 1) * P].rearrange("a r n -> (a r) n"),
                                     ys[32 * q:32 * q + 2 * HD, batch % 2, :]).then_inc(y_stored[batch % 2], 16)

            pipeline(sp, one)
            for s in range(2):
                sp.wait_ge(y_stored[s], 64 * (BLOCKS // 8) + 16)

        @block.gpsimd
        def _(pool):
            pool.memset(zeros[:], 0.0).then_inc(zeroed, 1)
            pool.memset(vs[:], 0.0).then_inc(zeroed, 1)
            pool.memset(f32(qs[:]), 0.0).then_inc(cleared, 1)
            for t_ in ks:
                pool.memset(f32(t_[:]), 0.0).then_inc(cleared, 1)
            pool.wait_ge(cleared, 3)
            pool.wait_ge(zeroed, 2)
            pool.memset(vs[:, :, :, HD:2 * HD], 1.0).then_inc(zeroed, 1)
            pool.wait_ge(zeroed, 3)

            def one(i, k):
                if there(k, 4):
                    x = k + 4
                    pool.wait_ge(hi_ready, 16 * i + x + 1)
                    rest = rel_rest[:, x % 4, :]
                    wait(pool, lo_ready, 16 * i + x - 3)
                    pool.tensor_tensor(rest, rel_raw[:, x % 4, :], rel_part[0][:, x % 8, :], ALU.subtract).then_inc(rest_ready, 1)
                if there(k, 3):
                    x = k + 3
                    rest = rel_rest[:, x % 4, :]
                    pool.wait_ge(mid_ready, 16 * i + x + 1)
                    pool.tensor_tensor(rel_part[2][:, x % 8, :], rest, rel_part[1][:, x % 8, :], ALU.subtract).then_inc(lo_ready, 1)
                if there(k) and k % NB == 2:
                    n = 2 * i + k // NB
                    wait(pool, pv_done, 16 * i + 8 * (k // NB) - 4)
                    pool.tensor_copy(vs[:, slot(k), :, 0:HD], sb["v"][:, bass.ds(n * (NB * HD), NB * HD)]
                                     .rearrange("p (j d) -> p j d", d=HD)).then_inc(v_ready, 1)

            pipeline(pool, one)

        @block.tensor
        def _(pe):
            pe.wait_ge(emb_ready, 2)

            def one(i, k):
                if there(k, 2):
                    x = k + 2
                    pe.wait_ge(max_ready, 16 * i + x + 1)
                    if there(k, 5):
                        pe.wait_ge(rel_saved, 16 * i + k + 6)
                    wait(pe, row_saved, 16 * i + x)
                    pe.matmul(max_row, negmax[:, x % 4:x % 4 + 1], ident, start=True, stop=True).then_inc(row_ready, 1)
                if there(k, 3):
                    x = k + 3
                    tile_i = x % NB
                    if x % NB == 0:
                        pe.wait_ge(k_loaded[slot(x)], 64 * i + 64 * (x // 16) + 64)
                    wait(pe, max_ready, 16 * i + x)
                    pe.wait_ge(hi_ready, 16 * i + x + 1)
                    for g in range(2):
                        rows = slice(64 * g, 64 * g + K3)
                        j0, j1 = 4 * g, 4 * g + 4
                        edge = min(max(tile_i + 2, j0), j1)
                        for kv, a, b in ((ks[1], edge, j1), (ks[0], j0, edge)):
                            if a < b:
                                ins = pe.matmul(s_ps[:, a * P:b * P], qs[rows, slot(x), tile_i * P:(tile_i + 1) * P],
                                                kv[rows, slot(x), (a - j0) * P:(b - j0) * P], start=True, stop=True)
                        a, b = max(tile_i - 1, j0), min(tile_i + 2, j1)
                        if a < b:
                            c = (a - tile_i + 1) * P
                            ins = pe.matmul(s_ps[:, a * P:b * P], ident_b[:], rel_part[0][:, x % 8, c:c + (b - a) * P],
                                            start=False, stop=True, skip_group_check=True)
                    ins.then_inc(s_ready, 1)
                if there(k):
                    even = k % NB - k % 2
                    if k % 2 == 0:
                        pe.wait_ge(row_saved, 16 * i + k + 2)
                        pe.wait_ge(lo_ready, 16 * i + k + 2)
                    pe.wait_ge(exp_done, 16 * i + k + 1)
                    g = k % 2
                    rows = slice(64 * g, 64 * g + MROW + 1)
                    for j in range(4 * g, 4 * g + 4):
                        both = [(0, 1), (1, 2)] if j == even + 2 else [(0, 2)]
                        band = [h for h in range(2) if abs(j - even - h) <= 1]
                        at = j % 4 * 2
                        for a, b in both:
                            kv = ks[0] if j <= even + b else ks[1]
                            ins = pe.matmul(st[k % 2][:, (at + a) * P:(at + b) * P], kv[rows, slot(k), j % 4 * P:(j % 4 + 1) * P],
                                            qs[rows, slot(k), (even + a) * P:(even + b) * P], start=True, stop=True)
                        for h in band:
                            c = (j - even - h + 1) * P
                            for part in rel_part:
                                ins = pe.matmul(st[k % 2][:, (at + h) * P:(at + h + 1) * P], part[:, (k - k % 2 + h) % 8, c:c + P], ident_b[:],
                                                start=False, stop=True, skip_group_check=True)
                    ins.then_inc(st_ready, 1)
                if there(k, 6):
                    x = k + 6
                    if x % NB == 0:
                        pe.wait_ge(q_loaded[slot(x)], 32 * i + 32 * (x // 16) + 32)
                    wait(pe, rel_saved, 16 * i + x)
                    wait(pe, row_saved, 16 * i + x - 3)
                    q = qs[0:K3, slot(x), x % NB * P:(x % NB + 1) * P]
                    pe.matmul(rel_ps[:, 0:BAND], q, emb_all[:], start=True, stop=True).then_inc(rel_ready, 1)
                if k >= 4:
                    batch, r = k // 4 - 1, k % 4
                    if r == 0:
                        pe.wait_ge(exp_done, 16 * i + k + 2)
                        pe.wait_ge(v_ready, 2 * i + batch // 2 + 1)
                        pe.wait_ge(y_saved, 4 * i + batch + 1)
                    for j in (2 * r, 2 * r + 1):
                        for q in range(4):
                            ins = pe.matmul(acc[32 * q:32 * q + 32, 0:P], vs[:, batch // 2 % 2, j, :],
                                            probs[:, (4 * batch + q - q % 2 + j // 4) % 8, (j % 4 * 2 + q % 2) * P:(j % 4 * 2 + q % 2 + 1) * P],
                                            start=(j == 0), stop=(j == NB - 1))
                    ins.then_inc(pv_done, 1)

            pipeline(pe, one)

        @block.scalar
        def _(act):
            act.sem_inc(exp_done, 2)

            def one(i, k):
                if there(k, 4):
                    x = k + 4
                    act.wait_ge(rel_read[x % 4], 64 * i + 16 * (x // 4) + 16)
                    wait(act, st_ready, 16 * i + x - 7)
                    act.activation(rel_part[0][:, x % 8, :], rel_raw[:, x % 4, :], ACT.Copy).then_inc(hi_ready, 1)
                if there(k):
                    act.wait_ge(st_ready, 16 * i + k + 1)
                    wait(act, pv_done, 16 * i + 4 * (k // 4))
                    act.activation(probs[:, k % 8, :], st[k % 2][:], ACT.Exp, scale=SCALE).then_inc(exp_done, 1)

            pipeline(act, one)

        @block.vector
        def _(dve):
            count = [0]

            def then(ins):
                count[0] += 1
                ins.then_inc(step, 1)
                dve.wait_ge(step, count[0])

            dve.sem_inc(y_saved, 1)
            dve.sem_inc(pv_done, 4)
            for s in range(2):
                dve.sem_inc(y_stored[s], 16)
            dve.tensor_copy(ident_b[:], ident).then_inc(emb_ready, 1)
            dve.wait_ge(cleared, 3)
            for t_ in ks:
                for g in range(2):
                    ins = dve.memset(f32(t_[64 * g + MROW:64 * g + MROW + 1, :, :]), 1.0)
            ins.then_inc(cleared, 1)
            dve.wait_ge(loaded, 48)
            then(dve.tensor_scalar(emb[:, 1, :], emb[:, 0, :], ecol[:, 0:1], None, ALU.subtract))
            then(dve.tensor_copy(emb_hi[:], emb[:, 1, :]))
            then(dve.tensor_tensor(emb[:, 2, :], emb[:, 1, :], f32(emb_hi[:]), ALU.subtract))
            then(dve.tensor_scalar(emb[:, 2, :], emb[:, 2, :], ecol[:, 1:2], None, ALU.mult))
            dve.scalar_tensor_tensor(emb_all[:], f32(emb_hi[:]), ecol[:, 2:3], emb[:, 2, :], ALU.mult, ALU.add).then_inc(emb_ready, 1)

            def one(i, k):
                if there(k, 2):
                    x = k + 2
                    dve.wait_ge(row_ready, 16 * i + x + 1)
                    for g in range(2):
                        row = 64 * g + MROW
                        ins = dve.tensor_copy(qs[row:row + 1, slot(x), x % NB * P:(x % NB + 1) * P], max_row)
                    ins.then_inc(row_saved, 1)
                if there(k, 3):
                    x = k + 3
                    dve.wait_ge(rest_ready, 16 * i + x + 1)
                    dve.tensor_copy(rel_part[1][:, x % 8, :], rel_rest[:, x % 4, :]).then_inc(mid_ready, 1)
                if there(k, 3):
                    x = k + 3
                    dve.wait_ge(s_ready, 16 * i + x + 1)
                    dve.tensor_reduce(negmax[:, x % 4:x % 4 + 1], s_ps[:], AX.X, ALU.max, negate=True).then_inc(max_ready, 1)
                if there(k, 6):
                    x = k + 6
                    dve.wait_ge(rel_ready, 16 * i + x + 1)
                    wait(dve, rel_written[x % 4], 64 * i + 16 * (x // 4))
                    dve.tensor_copy(rel_sb[:, x % 4, :], rel_ps[:, 0:BAND]).then_inc(rel_saved, 1)
                if k >= 4 and k % 4 == 3:
                    batch = k // 4 - 1
                    dve.wait_ge(pv_done, 16 * i + 4 * batch + 4 + 4)
                    dve.wait_ge(y_stored[batch % 2], 128 * i + 64 * (batch // 2) + 16)
                    dve.tensor_copy(ys[:, batch % 2, :], acc[:, 0:P]).then_inc(y_saved, 1)

            pipeline(dve, one)


def experts(nc, d, sb, scr, layer):
    k = layer.index
    E, CK = layer.E, layer.chunks
    K = len(CK)
    R = layer.rows
    with ExitStack() as ctx:
        def tile(name, shape, dt=F32):
            return ctx.enter_context(nc.sbuf_tensor(f"f{k}_{name}", shape, dt))

        def sem(name):
            return ctx.enter_context(nc.semaphore(f"f{k}_{name}"))

        GRP = 3
        groups = [(c, min(c + GRP, K)) for c in range(0, K, GRP)]
        raw = tile("raw", [P, 2, 4, GRP * P])
        wide = K * P
        w_hi = [tile(f"w{m}_hi", [P, wide], F32R) for m in (1, 3, 2)]
        w_lo = [tile(f"w{m}_lo", [P, wide], F32R) for m in (1, 3, 2)]
        sel = tile("sel", [P, wide], F32R)
        if k == 0:
            b1, b3 = tile("b1", [P, K]), tile("b3", [P, K])
            b2 = tile("b2", [P, D]); b2_hi = tile("b2_hi", [P, D], F32R); b2_lo = tile("b2_lo", [P, D], F32R)
        gate = tile("gate", [P, 2, CH]); up = tile("up", [P, 2, CH]); hid = tile("hid", [P, 2, CH])
        hid_hi = tile("hid_hi", [P, 4, CH], F32R); hid_lo = tile("hid_lo", [P, 4, CH], F32R)
        if k == 1:
            yv, ysum = sb["xn"], sb["v"]
            y_hi, y_lo = tile("y_hi", [P, N], F32R), tile("y_lo", [P, N], F32R)
            wp = tile("wp", [P, D]); wp_hi = tile("wp_hi", [P, D], F32R); wp_lo = tile("wp_lo", [P, D], F32R)
        else:
            yv = tile("yv", [P, N])
        yT = sb["yT"]

        def pb(name):
            return ctx.enter_context(nc.psum_tensor(f"f{k}_{name}", [P, CH], F32))
        g_ps, u_ps, c_ps = [pb(f"g{i}") for i in range(2)], [pb(f"u{i}") for i in range(2)], [pb(f"c{i}") for i in range(2)]
        y_ps, z_ps = pb("y"), pb("z")

        raw_loaded = [sem(f"raw_loaded{s}") for s in range(2)]
        raw_hi, raw_lo, w_ready = sem("raw_hi"), sem("raw_lo"), sem("w_ready")
        small, att_sorted, att_loaded, att_ready, step = sem("small"), sem("att_sorted"), sem("att_loaded"), sem("att_ready"), sem("step")
        bias_ready = sem("bias_ready")
        g_ready, u_ready, gate_ready, up_ready, hid_ready = sem("g_ready"), sem("u_ready"), sem("gate_ready"), sem("up_ready"), sem("hid_ready")
        hi_ready, lo_ready, down_done = sem("hi_ready"), sem("lo_ready"), sem("down_done")
        y_ready, turned, out_ready, out_stored = sem("y_ready"), sem("turned"), sem("out_ready"), sem("out_stored")
        names = [("w1", 0), ("w3", 1), ("w2", 2), ("sel", 3)]
        block = ctx.enter_context(nc.Block())

        def pieces(m, c0, c1):
            if m != 2:
                return [(P, c0 * P, min(c1 * P, R))]
            full = R // P
            parts = [(P, c0 * P, min(c1, full) * P), (R - full * P, max(c0, full) * P, c1 * P)]
            return [p for p in parts if p[2] > p[1]]

        @block.sync
        def _(sp):
            if k == 0:
                sp.dma_start(b1[:], d["b1"]).then_inc(small, 16)
                sp.dma_start(b3[:], d["b3"]).then_inc(small, 16)
                sp.dma_start(b2[0:E + 1, :], d["b2"]).then_inc(small, 16)
                sp.dma_start(b2[LO_ROW:LO_ROW + E + 1, :], d["b2"]).then_inc(small, 16)
                sp.dma_start(yv[:].rearrange("p (b t) -> p b t", b=B), scr["y0"]).then_inc(att_loaded, 16)
            else:
                sp.dma_start(wp[:], d["wproj"]).then_inc(small, 16)
                for w in range(2):
                    for b in range(B):
                        sp.dma_start(scr["y1c"][w, b], scr["y1"][w, b]).then_inc(att_sorted, 16)
                sp.wait_ge(att_sorted, 64)
                for w, t_ in enumerate((yv, ysum)):
                    sp.dma_start(flat(t_).rearrange("p (b t) -> p b t", b=B), scr["y1r"][w]).then_inc(att_loaded, 16)
            for n, (c0, c1) in enumerate(groups):
                s = n % 2
                if n >= 2:
                    sp.wait_ge(raw_lo, n - 1)
                for name, m in names:
                    for rows, a, b in pieces(m, c0, c1):
                        dst = raw[0:rows, s, m, a - c0 * P:b - c0 * P]
                        if m == 2:
                            sp.dma_start(dst.rearrange("p (c n) -> p c n", n=D),
                                         d[f"w2_{k}"][a:a + (b - a) // P * rows].rearrange("(c p) n -> p c n", p=rows)).then_inc(raw_loaded[s], 16)
                        else:
                            sp.dma_start(dst, d[f"{name}_{k}"][:, a:b]).then_inc(raw_loaded[s], 16)
            if k == 1:
                for t in range(NC):
                    sp.wait_ge(out_ready, t + 1)
                    sp.dma_start(d["out"].rearrange("(c t p) d -> c p t d", p=P, t=4)[t], sb["x"][:, 4 * t:4 * t + 4, :]).then_inc(out_stored, 16)
                sp.wait_ge(out_stored, 16 * NC)

        def raw_count(n):
            return sum(len(pieces(m, *groups[g])) for g in range(n % 2, n + 1, 2) for m in range(4))

        def split_hi(eng, n, copy):
            c0, c1 = groups[n]
            eng.wait_ge(raw_loaded[n % 2], 16 * raw_count(n))
            for m in range(4):
                for rows, a, b in pieces(m, c0, c1):
                    ins = copy((*w_hi, sel)[m][0:rows, a:b], raw[0:rows, n % 2, m, a - c0 * P:b - c0 * P])
            ins.then_inc(raw_hi, 1)

        def split_lo(eng, n):
            c0, c1 = groups[n]
            eng.wait_ge(raw_hi, n + 1)
            for m in range(3):
                for rows, a, b in pieces(m, c0, c1):
                    ins = eng.tensor_tensor(w_lo[m][0:rows, a:b], raw[0:rows, n % 2, m, a - c0 * P:b - c0 * P],
                                            f32(w_hi[m][0:rows, a:b]), ALU.subtract)
            ins.then_inc(raw_lo, 1)

        @block.tensor
        def _(pe):
            if k == 0:
                pe.wait_ge(bias_ready, 2)
            else:
                pe.wait_ge(att_ready, 2)
            with pe.Fori(0, NC) as ti:
                cols = bass.ds(ti * CH, CH)

                def rise(c):
                    n, m = ti * K + c, CK[c]
                    ch = slice(c * P, c * P + m)
                    if c == 0 or c % GRP == 0:
                        pe.wait_ge(raw_lo, c // GRP + 1)
                    pe.wait_ge(gate_ready, ti * K + max(c - 1, 0) + 1)
                    g, u, w = g_ps[c % 2][0:m, :], u_ps[c % 2][0:m, :], c_ps[c % 2][0:m, :]
                    pe.matmul(g, w_hi[0][:, ch], sb["x_hi"][:, cols], start=True, stop=False)
                    pe.matmul(g, w_lo[0][:, ch], sb["x_hi"][:, cols], start=False, stop=False)
                    pe.matmul(g, w_hi[0][:, ch], sb["x_lo"][:, cols], start=False, stop=True).then_inc(g_ready, 1)
                    pe.wait_ge(hid_ready, ti * K + max(c - 1, 0) + 1)
                    pe.matmul(u, w_hi[1][:, ch], sb["x_hi"][:, cols], start=True, stop=False)
                    pe.matmul(u, w_lo[1][:, ch], sb["x_hi"][:, cols], start=False, stop=False)
                    pe.matmul(u, w_hi[1][:, ch], sb["x_lo"][:, cols], start=False, stop=True)
                    pe.matmul(w, sel[:, ch], sb["cw_split"][:, cols], start=True, stop=True).then_inc(u_ready, 1)

                def fall(c):
                    n, m = ti * K + c, CK[c]
                    ch = slice(c * P, (c + 1) * P)
                    pe.wait_ge(hi_ready, n + 1)
                    pe.wait_ge(lo_ready, n + 1)
                    pe.matmul(y_ps[:], w_hi[2][0:m, ch], hid_hi[0:m, c % 4, :], start=False, stop=False)
                    pe.matmul(y_ps[:], w_lo[2][0:m, ch], hid_hi[0:m, c % 4, :], start=False, stop=False)
                    ins = pe.matmul(y_ps[:], w_hi[2][0:m, ch], hid_lo[0:m, c % 4, :], start=False, stop=(c == K - 1))
                    ins.then_inc(down_done, 1)

                pe.wait_ge(y_ready, ti + 1)
                if k == 0:
                    pe.matmul(y_ps[:], b2_hi[:], sb["cw_split"][:, cols], start=True, stop=False)
                    pe.matmul(y_ps[:], b2_lo[:], sb["cw_split"][:, cols], start=False, stop=False)
                else:
                    pe.matmul(y_ps[:], wp_hi[:], y_hi[:, cols], start=True, stop=False)
                    pe.matmul(y_ps[:], wp_lo[:], y_hi[:, cols], start=False, stop=False)
                    pe.matmul(y_ps[:], wp_hi[:], y_lo[:, cols], start=False, stop=False)
                for c in range(K + 2):
                    if c < K:
                        rise(c)
                    if c >= 2:
                        fall(c - 2)
            if k == 1:
                for t in range(NT):
                    if t % 4 == 0:
                        pe.wait_ge(y_ready, t // 4 + 2)
                    if t >= 8 and t % 4 == 0:
                        pe.wait_ge(out_ready, t // 4 - 1)
                    out = (z_ps, g_ps[0])[t // 4 % 2]
                    ins = pe.transpose(out[:, (t % 4) * P:(t % 4 + 1) * P], yT[:, t * P:(t + 1) * P], sb["const"][:, C_ID:C_ID + P])
                    if t % 4 == 3:
                        ins.then_inc(turned, 1)

        @block.scalar
        def _(act):
            for n in range(len(groups)):
                split_hi(act, n, lambda o, x: act.activation(o, x, ACT.Copy))
            act.sem_inc(gate_ready, 1)
            if k == 0:
                act.wait_ge(small, 64)
            with act.Fori(0, NC) as ti:
                for c in range(K + 1):
                    n = ti * K + c
                    if c < K:
                        m = CK[c]
                        act.wait_ge(g_ready, n + 1)
                        act.wait_ge(hid_ready, ti * K + max(c - 1, 0) + 1)
                        bias = {"bias": b1[0:m, c:c + 1]} if k == 0 else {}
                        act.activation(gate[0:m, c % 2, :], g_ps[c % 2][0:m, :], ACT.Silu, **bias).then_inc(gate_ready, 1)
                    if c >= 1:
                        c_ = c - 1
                        m = CK[c_]
                        act.wait_ge(hid_ready, ti * K + c_ + 2)
                        act.wait_ge(down_done, ti * K + max(c_ - 3, 0) + 1)
                        act.activation(hid_hi[0:m, c_ % 4, :], hid[0:m, c_ % 2, :], ACT.Copy).then_inc(hi_ready, 1)

        @block.gpsimd
        def _(pool):
            for n in range(len(groups)):
                split_lo(pool, n)
            with pool.Fori(0, NC) as ti:
                for c in range(K):
                    m = CK[c]
                    pool.wait_ge(hi_ready, ti * K + c + 1)
                    pool.tensor_tensor(hid_lo[0:m, c % 4, :], hid[0:m, c % 2, :], f32(hid_hi[0:m, c % 4, :]), ALU.subtract).then_inc(lo_ready, 1)

        @block.vector
        def _(dve):
            count = [0]

            def then(ins):
                count[0] += 1
                ins.then_inc(step, 1)
                dve.wait_ge(step, count[0])

            dve.sem_inc(hid_ready, 1)
            dve.sem_inc(y_ready, 1)
            dve.sem_inc(down_done, 1)
            if k == 0:
                then(dve.memset(b2_lo[:].bitcast(F32), 0.0))
                dve.wait_ge(small, 64)
                then(dve.memset(b2_hi[:].bitcast(F32), 0.0))
                for rows in (slice(0, E + 1), slice(LO_ROW, LO_ROW + E + 1)):
                    then(dve.tensor_copy(b2_hi[rows, :], b2[rows, :]))
                    dve.tensor_tensor(b2_lo[rows, :], b2[rows, :], f32(b2_hi[rows, :]), ALU.subtract).then_inc(bias_ready, 1)
                dve.wait_ge(att_loaded, 16)
            else:
                dve.wait_ge(small, 16)
                then(dve.tensor_copy(wp_hi[:], wp[:]))
                dve.tensor_tensor(wp_lo[:], wp[:], f32(wp_hi[:]), ALU.subtract).then_inc(att_ready, 1)
                dve.wait_ge(att_loaded, 32)
                then(dve.reciprocal(ysum[:], ysum[:]))
                then(dve.tensor_tensor(flat(yv), flat(yv), ysum[:], ALU.mult))
                then(dve.tensor_copy(y_hi[:], flat(yv)))
                dve.tensor_tensor(y_lo[:], flat(yv), f32(y_hi[:]), ALU.subtract).then_inc(att_ready, 1)
            with dve.Fori(0, NC) as ti:
                for c in range(K):
                    n, m = ti * K + c, CK[c]
                    dve.wait_ge(u_ready, n + 1)
                    dve.wait_ge(gate_ready, n + 2)
                    u, w, g = u_ps[c % 2][0:m, :], c_ps[c % 2][0:m, :], gate[0:m, c % 2, :]
                    if k == 0:
                        dve.scalar_tensor_tensor(up[0:m, c % 2, :], u, b3[0:m, c:c + 1], g, ALU.add, ALU.mult).then_inc(up_ready, 1)
                    else:
                        dve.tensor_tensor(up[0:m, c % 2, :], u, g, ALU.mult).then_inc(up_ready, 1)
                    dve.wait_ge(up_ready, n + 1)
                    if c >= 2:
                        dve.wait_ge(lo_ready, ti * K + c - 1)
                    dve.tensor_tensor(hid[0:m, c % 2, :], w, up[0:m, c % 2, :], ALU.mult).then_inc(hid_ready, 1)
                dve.wait_ge(down_done, ti * K + K + 1)
                cols = bass.ds(ti * CH, CH)
                if k == 0:
                    dve.tensor_tensor(yT[:, cols], y_ps[:], yv[:, cols], ALU.add).then_inc(y_ready, 1)
                else:
                    dve.tensor_copy(yT[:, cols], y_ps[:]).then_inc(y_ready, 1)
            if k == 1:
                for c in range(NC):
                    dve.wait_ge(turned, c + 1)
                    part = sb["x"][:, 4 * c:4 * c + 4, :]
                    bank = (z_ps, g_ps[0])[c % 2]
                    dve.tensor_tensor(part, bank[:].rearrange("p (t d) -> p t d", d=D), part, ALU.add).then_inc(out_ready, 1)


def two_layers(nc, d):
    with ExitStack() as ctx:
        def tile(name, shape, dt=F32):
            return ctx.enter_context(nc.sbuf_tensor(name, shape, dt))

        sb = {
            "const": tile("const", [P, C_ALL]),
            "x": tile("x", [P, NT, D]), "xn": tile("xn", [P, NT, D]),
            "x_hi": tile("x_hi", [P, N], F32R), "x_lo": tile("x_lo", [P, N], F32R),
            "v": tile("v", [P, N]),
            "cw_split": tile("cw_split", [P, N], F32R),
            "yT": tile("yT", [P, N]),
        }
        scr = {}
        for name in ("q0", "k0", "q1", "ka", "kb"):
            whole = nc.dram_tensor("scr_" + name, (TERMS, B, P, T), F32, kind="Internal").ap()
            scr[name] = whole.rearrange("w b p t -> w p b t")
            scr[name + "h"] = whole.rearrange("w b (h r) t -> w (b h) r t", r=HD)
        y0 = nc.dram_tensor("scr_y0", (B * H, HD, T), F32, kind="Internal").ap()
        scr["y0h"] = y0
        scr["y0"] = y0.rearrange("(b h) r t -> (h r) b t", b=B)
        y1 = nc.dram_tensor("scr_y1", (B * H, 2 * HD, T), F32, kind="Internal").ap()
        scr["y1s"] = y1
        scr["y1"] = y1.rearrange("(b h) (w r) t -> w b h r t", b=B, w=2)
        y1c = nc.dram_tensor("scr_y1c", (2, B, H, HD, T), F32, kind="Internal").ap()
        scr["y1c"] = y1c
        scr["y1r"] = y1c.rearrange("w b h r t -> w (h r) b t")
        scr["rel"] = nc.dram_tensor("scr_rel", (16, P, RELROW), F32, kind="Internal").ap()

        prepare(nc, d, sb, scr, L0)
        sigmoid_attention(nc, d, sb, scr)
        experts(nc, d, sb, scr, L0)
        prepare(nc, d, sb, scr, L1)
        softmax_attention(nc, d, sb, scr)
        experts(nc, d, sb, scr, L1)


def selection(layer, np):
    sel = np.zeros((P, layer.rows), np.float32)
    per = 64 if layer.index == 0 else 176
    for r in range(layer.rows):
        e = min(r // per, layer.E)
        sel[e, r] = sel[LO_ROW + e, r] = 1.0
    return sel


def constants(np):
    c = np.zeros((P, C_ALL), np.float32)
    c[:, C_ID:C_ID + P] = np.eye(P)
    c[:, C_CAUSAL:C_CAUSAL + P] = np.triu(np.ones((P, P)))
    c[:, C_IOTA:C_IOTA + 32] = np.arange(32)
    c[:, C_TRI8:C_TRI8 + 64] = np.tril(np.ones((8, 8)), -1).ravel()
    c[:, C_TRI4:C_TRI4 + 16] = np.tril(np.ones((4, 4)), -1).ravel()
    c[:, C_POW:C_POW + NT] = -0.5
    return c


def laid_out(inputs, np):
    a = {n: np.asarray(v) for n, v in inputs.items()}
    pos = a["L1_attn_pos_emb_k"]
    by_offset = np.concatenate([pos[RADIUS:], pos[:RADIUS], np.repeat(pos[RADIUS - 1:RADIUS], P, 0)]).T
    rows24 = np.zeros((TERMS * HD, 4), np.float32)
    rows24[:, 0] = np.tile(pos[RADIUS], TERMS)
    rows24[2 * HD:, 1] = 1.0
    rows24[:2 * HD, 2] = 1.0
    out = {
        "const": constants(np),
        "x": a["L0_attn_x"].reshape(N, D),
        "gw0": a["L0_ffn_gw"], "gb0": a["L0_ffn_gb"],
        "gw1": a["L1_ffn_gate_w"].T, "gb1": a["L1_ffn_gate_bias"],
        "bqk": np.stack([a["L0_attn_bv_q"].ravel(), a["L0_attn_bv_k"].ravel()], 1),
        "bv": a["L0_attn_bv_v"].ravel(),
        "w1_0": np.concatenate([a["L0_ffn_w1"].transpose(1, 0, 2).reshape(D, -1), a["L0_ffn_sw1"]], 1),
        "w3_0": np.concatenate([a["L0_ffn_w3"].transpose(1, 0, 2).reshape(D, -1), a["L0_ffn_sw3"]], 1),
        "w2_0": np.concatenate([a["L0_ffn_w2"].reshape(-1, D), a["L0_ffn_sw2"]]),
        "b1": np.concatenate([a["L0_ffn_b1"].ravel(), a["L0_ffn_sb1"]]).reshape(-1, P).T,
        "b3": np.concatenate([a["L0_ffn_b3"].ravel(), a["L0_ffn_sb3"]]).reshape(-1, P).T,
        "b2": np.concatenate([a["L0_ffn_b2"], a["L0_ffn_sb2"][None]]),
        "w1_1": np.concatenate([a["L1_ffn_gate_proj"].reshape(-1, D), a["L1_ffn_shared_gate_w"]]).T,
        "w3_1": np.concatenate([a["L1_ffn_up_proj"].reshape(-1, D), a["L1_ffn_shared_up_w"]]).T,
        "w2_1": np.concatenate([a["L1_ffn_down_proj"].transpose(0, 2, 1).reshape(-1, D), a["L1_ffn_shared_down_w"].T]),
        "sel_0": selection(L0, np), "sel_1": selection(L1, np),
        "wqkv": np.stack([a["L1_attn_Wq"].T, a["L1_attn_Wk"].T, a["L1_attn_Wv"].T], 1),
        "wproj": a["L1_attn_Wproj"].T,
        "ecol": np.stack([np.tile(pos[RADIUS], H), np.tile(pos[RADIUS - 1], H)], 1),
        "emb": np.tile(by_offset, (TERMS, 1)),
        "ecol24": rows24,
    }
    return {n: np.ascontiguousarray(v) for n, v in out.items()}


def kernel(**inputs):
    import numpy as _np
    import concourse.bacc as _bacc
    from concourse.bass_utils import run_bass_kernel_spmd as _run

    nc = _bacc.Bacc("TRN2", target_bir_lowering=False, num_devices=1)
    arrays, d = {}, {}
    for name, a in laid_out(inputs, _np).items():
        arrays[f"in_{name}"] = a
        d[name] = nc.dram_tensor(f"in_{name}", a.shape, mybir.dt.from_np(a.dtype), kind="ExternalInput").ap()
    d["out"] = nc.dram_tensor("out_0", (N, D), F32, kind="ExternalOutput").ap()
    two_layers(nc, d)
    r = _run(nc, [arrays], core_ids=[0])
    return r.results[0]["out_0"].reshape(B, T, D)
```

```python
from contextlib import ExitStack

import concourse.bass as bass
from concourse import mybir

F32 = mybir.dt.float32
F32R = mybir.dt.float32r
BF16 = mybir.dt.bfloat16
U32 = mybir.dt.uint32
ALU = mybir.AluOpType
ACT = mybir.ActivationFunctionType
AX = mybir.AxisListType

P = 128
B, T, D = 2, 1024, 128
N = B * T
NT = N // P
H, HD = 16, 8
NB = T // P
CH = 512
NC = N // CH
EPS = 1e-5
TERMS = 3
RADIUS = 128
BAND = 3 * P
RELROW = 4 * P

C_ID, C_CAUSAL, C_IOTA, C_TRI8, C_TRI4, C_POW = 0, 128, 256, 288, 352, 368
C_ALL = 384


class Layer:

    def __init__(self, index, experts, group, top_groups, rows):
        self.index, self.E, self.per_group, self.top_groups = index, experts, group, top_groups
        self.G = experts // group
        self.rows = rows
        self.chunks = [min(P, rows - c) for c in range(0, rows, P)]


L0 = Layer(0, 32, 4, 4, 32 * 64 + 128)
L1 = Layer(1, 16, 4, 2, 16 * 176 + 352)
TOP = 4
LO_ROW = 64


def view(ap, *free):
    return bass.AP(ap.tensor, ap.offset, [ap.ap[0], *[list(f) for f in free]])


def f32(ap):
    return ap.bitcast(F32)


def flat(t):
    ap = t[:]
    return ap if len(ap.shape) == 2 else ap.rearrange("p a b -> p (a b)")


class Router:
    def __init__(self, nc, ctx, layer):
        def tile(name, shape, dt=F32):
            return ctx.enter_context(nc.sbuf_tensor(f"r{layer.index}_{name}", shape, dt))

        def sem(name):
            return ctx.enter_context(nc.semaphore(f"r{layer.index}_{name}"))

        self.layer = layer
        E, G = layer.E, layer.G
        self.sc, self.masked = tile("sc", [P, NT, E]), tile("masked", [P, NT, E])
        self.pair, self.gs = tile("pair", [P, 6, NT * G]), tile("gs", [P, NT, G])
        self.cmp_a, self.cmp_b = tile("cmp_a", [P, NT, G * G]), tile("cmp_b", [P, NT, G * G])
        self.keep, self.keep1 = tile("keep", [P, NT, G]), tile("keep1", [P, NT, G])
        self.top, self.topi, self.topf = tile("top", [P, NT, 8]), tile("topi", [P, NT, 8], U32), tile("topf", [P, NT, 8])
        self.biased = tile("biased", [P, NT, E]) if layer.index == 1 else None
        self.hot, self.cw, self.rs = tile("hot", [P, 2, NT, E]), tile("cw", [P, NT, E + 1]), tile("rs", [P, 2, NT])
        self.cw_ready, self.cw_turned = sem("cw_ready"), sem("cw_turned")
        self.cw_hi_done, self.cw_done = sem("cw_hi_done"), sem("cw_done")


def choose(router, sb, dve, then, chosen):
    layer, k = router.layer, router.layer.index
    E, G, PG = layer.E, layer.G, layer.per_group
    sc, masked, pair, gs, cmp_a, cmp_b = router.sc, router.masked, router.pair, router.gs, router.cmp_a, router.cmp_b
    keep, keep1, top, topi, topf, hot, cw, rs = (router.keep, router.keep1, router.top, router.topi, router.topf,
                                                 router.hot, router.cw, router.rs)
    quad = chosen[:].rearrange("p t (g e) -> p (t g) e", e=PG)
    hi1, lo1, hi2, lo2, mx, mn = (pair[:, i, :] for i in range(6))
    dve.tensor_tensor(hi1, quad[:, :, 0], quad[:, :, 1], ALU.max)
    dve.tensor_tensor(lo1, quad[:, :, 0], quad[:, :, 1], ALU.min)
    dve.tensor_tensor(hi2, quad[:, :, 2], quad[:, :, 3], ALU.max)
    then(dve.tensor_tensor(lo2, quad[:, :, 2], quad[:, :, 3], ALU.min))
    yield
    dve.tensor_tensor(mx, hi1, hi2, ALU.max)
    then(dve.tensor_tensor(mn, hi1, hi2, ALU.min))
    yield
    then(dve.tensor_tensor(lo1, lo1, lo2, ALU.max))
    yield
    then(dve.tensor_tensor(mn, mn, lo1, ALU.max))
    yield
    then(dve.tensor_tensor(gs[:].rearrange("p t g -> p (t g)"), mx, mn, ALU.add))
    yield
    one, other = view(gs[:], [G, NT], [1, G], [0, G]), view(gs[:], [G, NT], [0, G], [1, G])
    square = [[G * G, NT], [G, G], [1, G]]
    tri = sb["const"][:, (C_TRI8 if G == 8 else C_TRI4):]
    then(dve.tensor_tensor(view(cmp_a[:], *square), other, one, ALU.is_equal))
    yield
    then(dve.tensor_tensor(cmp_a[:], cmp_a[:], view(tri, [0, NT], [1, G * G]), ALU.mult))
    yield
    then(dve.tensor_tensor(view(cmp_b[:], *square), other, one, ALU.is_gt))
    yield
    then(dve.tensor_tensor(cmp_a[:], cmp_a[:], cmp_b[:], ALU.add))
    yield
    then(dve.tensor_reduce(keep[:], view(cmp_a[:], *square), AX.X, ALU.add))
    yield
    then(dve.tensor_scalar(keep[:], keep[:], float(layer.top_groups), None, ALU.is_lt))
    yield
    kept = view(keep[:], [G, NT], [1, G], [0, PG])
    by_group = [[E, NT], [PG, G], [1, PG]]
    then(dve.tensor_tensor(view(masked[:], *by_group), view(chosen[:], *by_group), kept, ALU.mult))
    yield
    if k == 0:
        then(dve.tensor_scalar(keep1[:], keep[:], 1.0, None, ALU.subtract))
        yield
        then(dve.tensor_tensor(view(masked[:], *by_group), view(masked[:], *by_group),
                               view(keep1[:], [G, NT], [1, G], [0, PG]), ALU.add))
        yield
    else:
        then(dve.tensor_scalar(masked[:], masked[:], 0.0, None, ALU.add))
        yield
    for t in range(NT):
        ins = dve.max(top[:, t, :], masked[:, t, :])
    then(ins)
    yield
    for t in range(NT):
        ins = dve.max_index(topi[:, t, :], top[:, t, :], masked[:, t, :])
    then(ins)
    yield
    then(dve.tensor_copy(topf[:], topi[:]))
    yield
    iota = view(sb["const"][:, C_IOTA:], [0, NT], [1, E])
    for i in range(TOP):
        then(dve.tensor_tensor(hot[:, min(i, 1)], iota, view(topf[:, 0, i:], [8, NT], [0, E]), ALU.is_equal))
        yield
        if i:
            then(dve.tensor_tensor(hot[:, 0], hot[:, 0], hot[:, 1], ALU.add))
            yield
    dve.wait_ge(router.cw_done, 2)
    if k == 0:
        dve.tensor_tensor(cw[:, :, 0:E], hot[:, 0], sc[:], ALU.mult).then_inc(router.cw_ready, 1)
    else:
        then(dve.tensor_tensor(hot[:, 0], hot[:, 0], sc[:], ALU.mult))
        yield
        then(dve.tensor_reduce(rs[:, 0, :], hot[:, 0], AX.X, ALU.add))
        yield
        then(dve.tensor_scalar(rs[:, 0, :], rs[:, 0, :], 1e-20, None, ALU.add))
        yield
        then(dve.reciprocal(rs[:, 1, :], rs[:, 0, :]))
        yield
        dve.tensor_tensor(cw[:, :, 0:E], hot[:, 0], view(rs[:, 1, :], [1, NT], [0, E]), ALU.mult).then_inc(router.cw_ready, 1)


def weights_turned(router, sb, pe, banks):
    E = router.layer.E
    pe.wait_ge(router.cw_ready, 1)
    for t in range(NT):
        ins = pe.transpose(banks[t // 4][0:E + 1, (t % 4) * P:(t % 4 + 1) * P], router.cw[:, t, :], sb["const"][:, C_ID:C_ID + P])
        if t % 4 == 3:
            ins.then_inc(router.cw_turned, 1)


def weights_hi(router, sb, act, banks):
    E = router.layer.E
    for c in range(NC):
        act.wait_ge(router.cw_turned, c + 1)
        if c == 0:
            act.wait_ge(router.cw_done, 1)
        act.activation(sb["cw_split"][0:E + 1, c * CH:(c + 1) * CH], banks[c][0:E + 1, :], ACT.Copy).then_inc(router.cw_hi_done, 1)


def weights_lo(router, sb, dve, banks):
    E = router.layer.E
    for c in range(NC):
        cols = slice(c * CH, (c + 1) * CH)
        dve.wait_ge(router.cw_hi_done, c + 1)
        dve.tensor_tensor(sb["cw_split"][LO_ROW:LO_ROW + E + 1, cols], banks[c][0:E + 1, :],
                          f32(sb["cw_split"][0:E + 1, cols]), ALU.subtract).then_inc(router.cw_done, 1)


def prepare(nc, d, sb, scr, router):
    layer = router.layer
    k = layer.index
    with ExitStack() as ctx:
        def tile(name, shape, dt=F32):
            return ctx.enter_context(nc.sbuf_tensor(f"{name}_{k}", shape, dt))

        def sem(name):
            return ctx.enter_context(nc.semaphore(f"{name}_{k}"))

        E, G, PG = layer.E, layer.G, layer.per_group
        sq = tile("sq", [P, NT, D])
        stat = tile("stat", [P, 4, NT])
        gw = tile("gw", [P, E]); gw_hi = tile("gw_hi", [P, E], F32R); gw_lo = tile("gw_lo", [P, E], F32R)
        gb = tile("gb", [P, E])
        sc, cw, biased, rs = router.sc, router.cw, router.biased, router.rs
        bank = [ctx.enter_context(nc.psum_tensor(f"bank{i}_{k}", [P, CH], F32)) for i in range(8)]
        if k == 0:
            sgn = tile("sgn", [P, 2, 4]); sgv = tile("sgv", [P, 2, D])
            q_hi = tile("q_hi", [P, N], F32R); q_lo = tile("q_lo", [P, N], F32R)
        else:
            wqkv = tile("wqkv", [P, 3, D]); w_hi = tile("w_hi", [P, 3, D], F32R); w_lo = tile("w_lo", [P, 3, D], F32R)
            ecol = tile("ecol", [P, 2])
            q_hi = tile("q_hi", [P, N], F32R); q_lo = tile("q_lo", [P, N], F32R)
            k_hi = [tile(f"k_hi{v}", [P, N], F32R) for v in range(2)]
            k_lo = [tile(f"k_lo{v}", [P, N], F32R) for v in range(2)]

        loaded, x_loaded = sem("loaded"), sem("x_loaded")
        var_ready, rstd_ready, xn_ready = sem("var_ready"), sem("rstd_ready"), sem("xn_ready")
        turned, hi_ready, lo_ready = sem("turned"), sem("hi_ready"), sem("lo_ready")
        gw_ready, logits_ready, exp_in, exp_ready = sem("gw_ready"), sem("logits_ready"), sem("exp_in"), sem("exp_ready")
        step, stored, att_ready = sem("step"), sem("stored"), sem("att_ready")
        back, x_ready, w_ready, proj_ready, proj_hi, proj_used = (sem("back"), sem("x_ready"), sem("w_ready"),
                                                        sem("proj_ready"), sem("proj_hi"), sem("proj_used"))
        ident = sb["const"][:, C_ID:C_ID + P]
        xn, x_hi, x_lo = sb["xn"], sb["x_hi"], sb["x_lo"]
        block = ctx.enter_context(nc.Block())

        @block.sync
        def _(sp):
            if k == 0:
                sp.dma_start(sb["x"][:], d["x"].rearrange("(t p) d -> p t d", p=P)).then_inc(x_loaded, 16)
                sp.dma_start(sb["const"][:], d["const"]).then_inc(x_loaded, 16)
                sp.dma_start(gw[:], d["gw0"]).then_inc(loaded, 16)
                sp.dma_start(gb[:], d["gb0"].partition_broadcast(P)).then_inc(loaded, 16)
                sp.dma_start(sgn[:, 0, 0:2], d["bqk"]).then_inc(loaded, 16)
                sp.dma_start(sgv[:, 0, :], d["bv"].partition_broadcast(P)).then_inc(loaded, 16)
                for w, (src, ready, n) in enumerate(((x_hi, hi_ready, NC), (x_hi, hi_ready, NC), (x_lo, lo_ready, NC))):
                    sp.wait_ge(ready, n)
                    sp.dma_start(scr["k0"][w], f32(src[:]).rearrange("p (b t) -> p b t", b=B)).then_inc(stored, 16)
                for w, src in enumerate((q_hi, q_lo, q_hi)):
                    sp.wait_ge(att_ready, 2)
                    sp.dma_start(scr["q0"][w], f32(src[:]).rearrange("p (b t) -> p b t", b=B)).then_inc(stored, 16)
                sp.wait_ge(stored, 16 * 6)
            else:
                sp.dma_start(gw[:], d["gw1"]).then_inc(loaded, 16)
                sp.dma_start(gb[:], d["gb1"].partition_broadcast(P)).then_inc(loaded, 16)
                sp.dma_start(wqkv[:], d["wqkv"]).then_inc(loaded, 16)
                sp.dma_start(ecol[:], d["ecol"]).then_inc(loaded, 16)
                n = 0
                for name, hi, lo, order in (("q1", q_hi, q_lo, "hlh"), ("ka", k_hi[0], k_lo[0], "hhl"),
                                            ("kb", k_hi[1], k_lo[1], "hhl")):
                    sp.wait_ge(proj_used, NC if name == "q1" else 2 * NC)
                    for w, part in enumerate(order):
                        src = hi if part == "h" else lo
                        sp.dma_start(scr[name][w], f32(src[:]).rearrange("p (b t) -> p b t", b=B)).then_inc(stored, 16)
                        n += 1
                sp.wait_ge(stored, 16 * n)

        @block.tensor
        def _(pe):
            if k == 1:
                for t in range(NT):
                    ins = pe.transpose(bank[t // 4][:, (t % 4) * P:(t % 4 + 1) * P], sb["yT"][:, t * P:(t + 1) * P], ident)
                    if t % 4 == 3:
                        ins.then_inc(back, 1)
                pe.wait_ge(x_ready, NC)
            pe.wait_ge(x_loaded, 32) if k == 0 else None
            pe.wait_ge(xn_ready, 1)
            for t in range(NT):
                ins = pe.transpose(bank[t // 4][:, (t % 4) * P:(t % 4 + 1) * P], xn[:, t, :], ident)
                if t % 4 == 3:
                    ins.then_inc(turned, 1)
            pe.wait_ge(gw_ready, 2)
            for t in range(NT):
                if t % 4 == 0:
                    pe.wait_ge(lo_ready, t // 4 + 1)
                    pe.wait_ge(hi_ready, t // 4 + 1)
                cols = slice(t * P, (t + 1) * P)
                out = bank[4][:, t * E:(t + 1) * E]
                pe.matmul(out, x_hi[:, cols], gw_hi[:], start=True, stop=False)
                pe.matmul(out, x_lo[:, cols], gw_hi[:], start=False, stop=False)
                ins = pe.matmul(out, x_hi[:, cols], gw_lo[:], start=False, stop=True)
            ins.then_inc(logits_ready, 1)
            if k == 1:
                pe.wait_ge(w_ready, 2)
                n = 0
                for w in range(2):
                    for c in range(NC):
                        if n >= 2:
                            pe.wait_ge(proj_used, n - 1)
                        out, cols = bank[5 + n % 2][:], slice(c * CH, (c + 1) * CH)
                        pe.matmul(out, w_hi[:, w, :], x_hi[:, cols], start=True, stop=False)
                        pe.matmul(out, w_lo[:, w, :], x_hi[:, cols], start=False, stop=False)
                        pe.matmul(out, w_hi[:, w, :], x_lo[:, cols], start=False, stop=True).then_inc(proj_ready, 1)
                        n += 1
                for t in range(NT):
                    if t % 4 == 0 and t >= 4:
                        pe.wait_ge(proj_used, 2 * NC + t // 4 - 1 if t >= 8 else 2 * NC)
                    out, cols = bank[(7, 5)[t // 4 % 2]][:, (t % 4) * P:(t % 4 + 1) * P], slice(t * P, (t + 1) * P)
                    pe.matmul(out, x_hi[:, cols], w_hi[:, 2, :], start=True, stop=False)
                    pe.matmul(out, x_lo[:, cols], w_hi[:, 2, :], start=False, stop=False)
                    ins = pe.matmul(out, x_hi[:, cols], w_lo[:, 2, :], start=False, stop=True)
                    if t % 4 == 3:
                        ins.then_inc(proj_ready, 1)
        @block.scalar
        def _(act):
            for c in range(NC):
                act.wait_ge(turned, c + 1)
                act.activation(x_hi[:, c * CH:(c + 1) * CH], bank[c][:], ACT.Copy).then_inc(hi_ready, 1)
            act.wait_ge(exp_in, 1)
            act.activation(sc[:], sc[:], ACT.Exp if k == 0 else ACT.Sigmoid).then_inc(exp_ready, 1)
            if k == 1:
                for c in range(NC):
                    act.wait_ge(proj_ready, c + 1)
                    act.activation(q_hi[:, c * CH:(c + 1) * CH], bank[5 + c % 2][:], ACT.Copy).then_inc(proj_hi, 1)
        @block.gpsimd
        def _(pool):
            pool.memset(f32(sb["cw_split"][:]), 0.0).then_inc(router.cw_done, 1)
            pool.memset(cw[:, :, E:E + 1], 1.0).then_inc(router.cw_done, 1)
            if k == 0:
                pool.wait_ge(x_loaded, 32)
            pool.wait_ge(var_ready, 1)
            pool.tensor_tensor(stat[:, 3, :], stat[:, 2, :], sb["const"][:, C_POW:C_POW + NT], ALU.pow).then_inc(rstd_ready, 1)

        @block.vector
        def _(dve):
            count = [0]

            def then(ins):
                count[0] += 1
                ins.then_inc(step, 1)
                dve.wait_ge(step, count[0])

            def per_tile(ap):
                return view(ap, [1, NT], [0, D])

            x = sb["x"]
            if k == 0:
                dve.wait_ge(x_loaded, 32)
            else:
                for c in range(NC):
                    dve.wait_ge(back, c + 1)
                    part = x[:, 4 * c:4 * c + 4, :]
                    dve.tensor_tensor(part, bank[c][:].rearrange("p (t d) -> p t d", d=D), part, ALU.add).then_inc(x_ready, 1)
                dve.wait_ge(x_ready, NC)
            then(dve.tensor_reduce(stat[:, 0, :], x[:], AX.X, ALU.add))
            then(dve.tensor_scalar(stat[:, 1, :], stat[:, 0, :], 1.0 / D, None, ALU.mult))
            then(dve.tensor_tensor(xn[:], x[:], per_tile(stat[:, 1, :]), ALU.subtract))
            then(dve.tensor_tensor(sq[:], xn[:], xn[:], ALU.mult))
            then(dve.tensor_reduce(stat[:, 0, :], sq[:], AX.X, ALU.add))
            dve.tensor_scalar(stat[:, 2, :], stat[:, 0, :], 1.0 / D, EPS, ALU.mult, ALU.add).then_inc(var_ready, 1)
            dve.wait_ge(loaded, 64)
            then(dve.tensor_copy(gw_hi[:], gw[:]))
            dve.tensor_tensor(gw_lo[:], gw[:], f32(gw_hi[:]), ALU.subtract).then_inc(gw_ready, 2)
            dve.wait_ge(rstd_ready, 1)
            dve.tensor_tensor(xn[:], xn[:], per_tile(stat[:, 3, :]), ALU.mult).then_inc(xn_ready, 1)
            if k == 0:
                then(dve.tensor_scalar(sgn[:, 1, 0:2], sgn[:, 0, 0:2], 0.0, None, ALU.is_gt))
                then(dve.tensor_scalar(sgn[:, 1, 2:4], sgn[:, 0, 0:2], 0.0, None, ALU.is_lt))
                then(dve.tensor_tensor(sgn[:, 0, 0:2], sgn[:, 1, 0:2], sgn[:, 1, 2:4], ALU.subtract))
                then(dve.tensor_tensor(sgn[:, 0, 2:3], sgn[:, 0, 0:1], sgn[:, 0, 1:2], ALU.mult))
                then(dve.tensor_scalar(sgv[:, 1, :], sgv[:, 0, :], 0.0, None, ALU.is_gt))
                then(dve.tensor_scalar(sgv[:, 0, :], sgv[:, 0, :], 0.0, None, ALU.is_lt))
                then(dve.tensor_tensor(sgv[:, 1, :], sgv[:, 1, :], sgv[:, 0, :], ALU.subtract))
                dve.wait_ge(xn_ready, 1)
                for b in range(B):
                    out = view(sb["v"][:, b * NB * D:], [HD, NB], [NB * HD, H], [1, HD])
                    src = view(xn[:, b * NB, :], [D, NB], [HD, H], [1, HD])
                    dve.tensor_tensor(out, src, view(sgv[:, 1, :], [0, NB], [HD, H], [1, HD]), ALU.mult)
            else:
                then(dve.tensor_copy(w_hi[:], wqkv[:]))
                dve.tensor_tensor(w_lo[:], wqkv[:], f32(w_hi[:]), ALU.subtract).then_inc(w_ready, 2)
            for c in range(NC):
                cols = slice(c * CH, (c + 1) * CH)
                dve.wait_ge(hi_ready, c + 1)
                dve.tensor_tensor(x_lo[:, cols], bank[c][:], f32(x_hi[:, cols]), ALU.subtract).then_inc(lo_ready, 1)
            if k == 0:
                dve.wait_ge(lo_ready, NC)
                dve.tensor_scalar(q_hi[:], f32(x_hi[:]), sgn[:, 0, 2:3], None, ALU.mult).then_inc(att_ready, 1)
                dve.tensor_scalar(q_lo[:], f32(x_lo[:]), sgn[:, 0, 2:3], None, ALU.mult).then_inc(att_ready, 1)
            dve.wait_ge(logits_ready, 1)
            logits = bank[4][:, 0:NT * E].rearrange("p (t e) -> p t e", e=E)
            if k == 0:
                then(dve.tensor_tensor(sc[:], logits, view(gb[:], [0, NT], [1, E]), ALU.add))
                then(dve.tensor_reduce(rs[:, 0, :], sc[:], AX.X, ALU.max))
                dve.tensor_tensor(sc[:], sc[:], view(rs[:, 0, :], [1, NT], [0, E]), ALU.subtract).then_inc(exp_in, 1)
                dve.wait_ge(exp_ready, 1)
                then(dve.tensor_reduce(rs[:, 0, :], sc[:], AX.X, ALU.add))
                then(dve.reciprocal(rs[:, 1, :], rs[:, 0, :]))
                then(dve.tensor_tensor(sc[:], sc[:], view(rs[:, 1, :], [1, NT], [0, E]), ALU.mult))
            else:
                dve.tensor_copy(sc[:], logits).then_inc(exp_in, 1)
                for c in range(NC):
                    cols = slice(c * CH, (c + 1) * CH)
                    dve.wait_ge(proj_hi, c + 1)
                    dve.tensor_tensor(q_lo[:, cols], bank[5 + c % 2][:], f32(q_hi[:, cols]), ALU.subtract).then_inc(proj_used, 1)
                for c in range(NC):
                    cols = slice(c * CH, (c + 1) * CH)
                    src = bank[5 + (NC + c) % 2][:]
                    dve.wait_ge(proj_ready, NC + c + 1)
                    for v in range(2):
                        then(dve.tensor_scalar(k_hi[v][:, cols], src, ecol[:, v:v + 1], None, ALU.add))
                    for v in range(2):
                        ins = dve.scalar_tensor_tensor(k_lo[v][:, cols], src, ecol[:, v:v + 1], f32(k_hi[v][:, cols]), ALU.add, ALU.subtract)
                    ins.then_inc(proj_used, 1)
                for c in range(NC):
                    dve.wait_ge(proj_ready, 2 * NC + c + 1)
                    b, j0 = c // 2, 4 * (c % 2)
                    out = view(sb["v"][:, b * NB * D + j0 * HD:], [HD, 4], [NB * HD, H], [1, HD])
                    src = view(bank[(7, 5)[c % 2]][:], [D, 4], [HD, H], [1, HD])
                    dve.tensor_copy(out, src).then_inc(proj_used, 1)
                dve.wait_ge(exp_ready, 1)
                then(dve.tensor_tensor(biased[:], sc[:], view(gb[:], [0, NT], [1, E]), ALU.add))


def sigmoid_attention(nc, d, sb, scr, router):
    SCALE = 4.0 * HD ** -0.5
    HALF, QUARTER = T // 2, T // 4
    PAIRS = B * H // 2
    with ExitStack() as ctx:
        def tile(name, shape, dt=F32):
            return ctx.enter_context(nc.sbuf_tensor("a0_" + name, shape, dt))

        def sem(name):
            return ctx.enter_context(nc.semaphore("a0_" + name))

        qs = tile("q", [P, 2, HALF], F32R)
        ks = tile("k", [P, 2, T], F32R)
        vs = tile("v", [P, 2, NB, 32])
        probs = tile("probs", [P, 4, T])
        ys = tile("y", [P, 2, QUARTER])
        st = [ctx.enter_context(nc.psum_tensor(f"a0_st{i}", [P, T], F32)) for i in range(2)]
        acc = [ctx.enter_context(nc.psum_tensor(f"a0_acc{i}", [P, CH], F32)) for i in range(2)]

        qk_loaded = [sem(f"qk_loaded{s}") for s in range(2)]
        y_stored = [sem(f"y_stored{s}") for s in range(2)]
        cleared, v_ready, st_ready, masked = sem("cleared"), sem("v_ready"), sem("st_ready"), sem("masked")
        passed = sem("passed")
        sig_done = sem("sig_done")
        probs_used = sem("probs_used")
        y_saved = sem("y_saved")
        step = sem("step")
        banks = [st[c // 2][:, c % 2 * CH:(c % 2 + 1) * CH] for c in range(NC)]
        block = ctx.enter_context(nc.Block())

        @block.sync
        def _(sp):
            def load(n, s):
                for g in range(2):
                    rows = slice(64 * g, 64 * g + TERMS * HD)
                    sp.dma_start(f32(qs[rows, s, :]), scr["q0h"][:, bass.ds(n, 1), :, g * HALF:(g + 1) * HALF]
                                 .rearrange("w a r t -> w (a r) t")).then_inc(qk_loaded[s], 16)
                    sp.dma_start(f32(ks[rows, s, :]), scr["k0h"][:, bass.ds(n, 1)]
                                 .rearrange("w a r t -> w (a r) t")).then_inc(qk_loaded[s], 16)

            def store(n, s):
                sp.wait_ge(y_saved, n + 3)
                sp.sem_inc(passed, 1)
                for r in range(4):
                    sp.dma_start(scr["y0h"][bass.ds(n, 1), :, r * QUARTER:(r + 1) * QUARTER].rearrange("a r t -> (a r) t"),
                                 ys[32 * r:32 * r + HD, s, :]).then_inc(y_stored[s], 16)

            for s in range(2):
                load(s, s)
            with sp.Fori(0, PAIRS - 1) as i:
                for s in range(2):
                    sp.wait_ge(st_ready, 16 * i + 8 * s + 8)
                    sp.sem_inc(passed, 1)
                    load(2 * i + s + 2, s)
                    store(2 * i + s, s)
            for s in range(2):
                store(2 * PAIRS - 2 + s, s)
            for s in range(2):
                sp.wait_ge(y_stored[s], 64 * PAIRS + 16)

        @block.gpsimd
        def _(pool):

            def copy_v(n, s):
                pool.tensor_copy(vs[:, s, :, 0:HD], sb["v"][:, bass.ds(n * (NB * HD), NB * HD)]
                                 .rearrange("p (j d) -> p j d", d=HD)).then_inc(v_ready, 1)

            def mask(i, t):
                j = t % NB
                pool.wait_ge(sig_done, 16 * i + t + 3)
                part = probs[:, j % 4, j * P:(j + 1) * P]
                pool.tensor_tensor(part, part, sb["const"][:, C_CAUSAL:C_CAUSAL + P], ALU.mult).then_inc(masked, 1)

            pool.memset(vs[:], 0.0).then_inc(cleared, 1)
            pool.wait_ge(cleared, 1)
            for s in range(2):
                copy_v(s, s)
            for t in range(2):
                mask(0, t)
            with pool.Fori(0, PAIRS - 1) as i:
                for t in range(2 * NB):
                    mask(i, t + 2)
                    if t % NB == NB - 1:
                        pool.wait_ge(probs_used, 16 * i + t + 1 + 4)
                        copy_v(2 * i + t // NB + 2, t // NB)
            for t in range(2, 2 * NB):
                mask(PAIRS - 1, t)

        @block.tensor
        def _(pe):
            def scores(i, t):
                s, j = t // NB % 2, t % NB
                if j == 0:
                    pe.wait_ge(qk_loaded[s], 64 * i + 64 * (t // (2 * NB)) + 64)
                pe.wait_ge(sig_done, 16 * i + t + 1)
                for g in range(2):
                    lo = max(j * P - g * HALF, 0)
                    if lo < HALF:
                        rows = slice(64 * g, 64 * g + TERMS * HD)
                        ins = pe.matmul(st[j % 2][:, g * HALF + lo:(g + 1) * HALF], ks[rows, s, j * P:(j + 1) * P],
                                        qs[rows, s, lo:HALF], start=True, stop=True)
                ins.then_inc(st_ready, 1)

            def values(i, t):
                s, j = t // NB, t % NB
                if j == 0:
                    pe.wait_ge(v_ready, 2 * i + s + 1)
                    pe.wait_ge(y_saved, 2 * i + s + 1)
                pe.wait_ge(masked, 16 * i + t + 1)
                for r in range(4):
                    lo = max(j * P - r * QUARTER, 0)
                    if lo < QUARTER:
                        ins = pe.matmul(acc[s][32 * r:32 * r + 32, lo:QUARTER], vs[:, s, j, :],
                                        probs[:, j % 4, r * QUARTER + lo:(r + 1) * QUARTER],
                                        start=(j == 0), stop=(j == 2 * r + 1))
                ins.then_inc(probs_used, 1)

            scores(0, 0)
            scores(0, 1)
            with pe.Fori(0, PAIRS - 1) as i:
                for t in range(2 * NB):
                    scores(i, t + 2)
                    values(i, t)
            for t in range(2 * NB):
                if t + 2 < 2 * NB:
                    scores(PAIRS - 1, t + 2)
                values(PAIRS - 1, t)
            pe.wait_ge(sig_done, 8 * B * H + 2)
            weights_turned(router, sb, pe, banks)

        @block.scalar
        def _(act):
            act.sem_inc(sig_done, 2)
            with act.Fori(0, PAIRS // 4) as i:
                for t in range(8 * NB):
                    j = t % NB
                    act.wait_ge(st_ready, 64 * i + t + 1)
                    act.wait_ge(probs_used, 64 * i + t + 1)
                    act.activation(probs[:, j % 4, j * P:], st[j % 2][:, j * P:], ACT.Sigmoid, scale=SCALE).then_inc(sig_done, 1)
            weights_hi(router, sb, act, banks)

        @block.vector
        def _(dve):
            count = [0]

            def then(ins):
                count[0] += 1
                ins.then_inc(step, 1)
                dve.wait_ge(step, count[0])

            dve.sem_inc(y_saved, 2)
            dve.sem_inc(probs_used, 4)
            for s in range(2):
                dve.sem_inc(y_stored[s], 16)
            for _ in choose(router, sb, dve, then, router.sc):
                pass
            with dve.Fori(0, PAIRS) as i:
                for s in range(2):
                    dve.wait_ge(probs_used, 16 * i + 8 * s + 8 + 4)
                    dve.wait_ge(y_stored[s], 64 * i + 16)
                    dve.tensor_copy(ys[:, s, :], acc[s][:, 0:QUARTER]).then_inc(y_saved, 1)
            weights_lo(router, sb, dve, banks)


def softmax_attention(nc, d, sb, scr, router):
    SCALE = HD ** -0.5
    K3 = TERMS * HD
    MROW = 32
    LEAD = 6
    BLOCKS = B * H * NB
    RD = 16
    with ExitStack() as ctx:
        def tile(name, shape, dt=F32):
            return ctx.enter_context(nc.sbuf_tensor("a1_" + name, shape, dt))

        def sem(name):
            return ctx.enter_context(nc.semaphore("a1_" + name))

        qs = tile("q", [P, 2, T], F32R)
        ks = [tile(n, [P, 2, T // 2], F32R) for n in ("ka", "kb")]
        vs = tile("v", [P, 2, NB, 32])
        probs = tile("probs", [P, 8, T])
        rel_sb = tile("rel", [P, 4, BAND]); rel_raw = tile("rel_raw", [P, 4, BAND])
        rel_part = [tile(f"rel_part{n}", [P, 8, BAND], BF16) for n in range(3)]
        rel_rest = tile("rel_rest", [P, 4, BAND])
        negmax = tile("negmax", [P, 4]); ys = tile("y", [P, 2, P])
        ident_b = tile("ident_b", [P, P], BF16)
        emb = tile("emb", [K3, 3, BAND]); emb_hi = tile("emb_hi", [K3, BAND], F32R); emb_all = tile("emb_all", [K3, BAND], F32R)
        ecol = tile("ecol", [K3, 4]); zeros = tile("zeros", [P, P])
        s_ps = ctx.enter_context(nc.psum_tensor("a1_s_ps", [P, T], F32))
        rel_ps = ctx.enter_context(nc.psum_tensor("a1_rel_ps", [P, CH], F32))
        acc = ctx.enter_context(nc.psum_tensor("a1_acc_ps", [P, CH], F32))
        st = [ctx.enter_context(nc.psum_tensor(f"a1_st_ps{i}", [P, T], F32)) for i in range(2)]
        ident = sb["const"][:, C_ID:C_ID + P]
        max_row = rel_ps[0:1, BAND:BAND + P]

        loaded, cleared, step, emb_ready, zeroed = sem("loaded"), sem("cleared"), sem("step"), sem("emb_ready"), sem("zeroed")
        q_loaded = [sem(f"q_loaded{s}") for s in range(2)]
        k_loaded = [sem(f"k_loaded{s}") for s in range(2)]
        rel_written = [sem(f"rel_written{s}") for s in range(4)]
        rel_read = [sem(f"rel_read{s}") for s in range(4)]
        y_stored = [sem(f"y_stored{s}") for s in range(2)]
        rel_ready, rel_saved, hi_ready, lo_ready = sem("rel_ready"), sem("rel_saved"), sem("hi_ready"), sem("lo_ready")
        s_ready, max_ready, row_ready, row_saved = sem("s_ready"), sem("max_ready"), sem("row_ready"), sem("row_saved")
        st_ready, v_ready = sem("st_ready"), sem("v_ready")
        passed = sem("passed")
        rest_ready, mid_ready = sem("rest_ready"), sem("mid_ready")
        exp_done = sem("exp_done")
        pv_done = sem("pv_done")
        y_saved = sem("y_saved")

        def wait(eng, s, value):
            if not isinstance(value, int) or value > 0:
                eng.wait_ge(s, value)

        def pipeline(eng, one):
            for k in range(-LEAD, 4):
                one(0, k)
            with eng.Fori(0, BLOCKS // 16 - 1) as i:
                for k in range(4, 20):
                    one(i, k)
            for k in range(BLOCKS - 12, BLOCKS + 4):
                one(0, k)

        def there(k, lead=0):
            return 0 <= k + lead < BLOCKS

        def slot(k):
            return k // NB % 2

        banks = [st[c // 2][:, c % 2 * CH:(c % 2 + 1) * CH] for c in range(NC)]
        block = ctx.enter_context(nc.Block())

        @block.sync
        def _(sp):
            sp.dma_start(emb[:, 0, :], d["emb"]).then_inc(loaded, 16)
            sp.dma_start(ecol[:], d["ecol24"]).then_inc(loaded, 16)
            sp.wait_ge(zeroed, 1)
            sp.dma_start(scr["rel"][:, :, 0:P - 1].rearrange("s p u -> p s u"), view(zeros[:], [0, RD], [1, P - 1])).then_inc(loaded, 16)
            sp.wait_ge(loaded, 48)
            sp.wait_ge(cleared, 4)

            def load(name, dst, n, s, loaded):
                for g in range(2):
                    src = scr[name][:, bass.ds(n, 1)]
                    if name != "q1h":
                        src = src[:, :, :, g * (T // 2):(g + 1) * (T // 2)]
                    sp.dma_start(f32(dst[64 * g:64 * g + K3, s, :]), src.rearrange("w a r t -> w (a r) t")).then_inc(loaded[s], 16)

            def one(i, k):
                if k == -LEAD:
                    load("q1h", qs, 0, 0, q_loaded)
                    load("kah", ks[0], 0, 0, k_loaded)
                    load("kbh", ks[1], 0, 0, k_loaded)
                if there(k, 5):
                    x = k + 5
                    sp.wait_ge(rel_written[x % 4], 64 * i + 16 * (x // 4) + 16)
                    sp.sem_inc(passed, 1)
                    wait(sp, lo_ready, 16 * i + x - 3)
                    sp.sem_inc(passed, 1)
                    row = scr["rel"][x % RD]
                    skewed = bass.AP(row.tensor, row.offset + P - 1, [[RELROW - 1, P], [1, BAND]])
                    sp.dma_start(rel_raw[:, x % 4, :], skewed).then_inc(rel_read[x % 4], 16)
                if there(k, 6):
                    x = k + 6
                    sp.wait_ge(rel_saved, 16 * i + x + 1)
                    sp.sem_inc(passed, 1)
                    sp.dma_start(scr["rel"][x % RD, :, P - 1:P - 1 + BAND], rel_sb[:, x % 4, :]).then_inc(rel_written[x % 4], 16)
                if k >= 0 and k - k % NB + NB < BLOCKS and k % NB < 3:
                    first = k - k % NB
                    if k == first:
                        wait(sp, st_ready, 16 * i + k)
                        sp.sem_inc(passed, 1)
                    name, dst, loaded_ = (("q1h", qs, q_loaded), ("kah", ks[0], k_loaded), ("kbh", ks[1], k_loaded))[k % NB]
                    load(name, dst, 2 * i + k // NB + 1, slot(k + NB), loaded_)
                if k >= 4 and k % 4 == 3:
                    batch = k // 4 - 1
                    sp.wait_ge(y_saved, 4 * i + batch + 2)
                    sp.sem_inc(passed, 1)
                    for q in range(4):
                        tile_i = batch % 2 * 4 + q
                        sp.dma_start(scr["y1s"][bass.ds(2 * i + batch // 2, 1), :, tile_i * P:(tile_i + 1) * P].rearrange("a r n -> (a r) n"),
                                     ys[32 * q:32 * q + 2 * HD, batch % 2, :]).then_inc(y_stored[batch % 2], 16)

            pipeline(sp, one)
            for s in range(2):
                sp.wait_ge(y_stored[s], 64 * (BLOCKS // 8) + 16)

        @block.gpsimd
        def _(pool):
            pool.memset(zeros[:], 0.0).then_inc(zeroed, 1)
            pool.memset(vs[:], 0.0).then_inc(zeroed, 1)
            pool.memset(f32(qs[:]), 0.0).then_inc(cleared, 1)
            for t_ in ks:
                pool.memset(f32(t_[:]), 0.0).then_inc(cleared, 1)
            pool.wait_ge(cleared, 3)
            pool.wait_ge(zeroed, 2)
            pool.memset(vs[:, :, :, HD:2 * HD], 1.0).then_inc(zeroed, 1)
            pool.wait_ge(zeroed, 3)

            def one(i, k):
                if there(k, 4):
                    x = k + 4
                    pool.wait_ge(hi_ready, 16 * i + x + 1)
                    rest = rel_rest[:, x % 4, :]
                    wait(pool, lo_ready, 16 * i + x - 3)
                    pool.tensor_tensor(rest, rel_raw[:, x % 4, :], rel_part[0][:, x % 8, :], ALU.subtract).then_inc(rest_ready, 1)
                if there(k, 3):
                    x = k + 3
                    rest = rel_rest[:, x % 4, :]
                    pool.wait_ge(mid_ready, 16 * i + x + 1)
                    pool.tensor_tensor(rel_part[2][:, x % 8, :], rest, rel_part[1][:, x % 8, :], ALU.subtract).then_inc(lo_ready, 1)
                if there(k) and k % NB == 2:
                    n = 2 * i + k // NB
                    wait(pool, pv_done, 16 * i + 8 * (k // NB) - 4)
                    pool.tensor_copy(vs[:, slot(k), :, 0:HD], sb["v"][:, bass.ds(n * (NB * HD), NB * HD)]
                                     .rearrange("p (j d) -> p j d", d=HD)).then_inc(v_ready, 1)

            pipeline(pool, one)

        @block.tensor
        def _(pe):
            pe.wait_ge(emb_ready, 2)

            def one(i, k):
                if there(k, 2):
                    x = k + 2
                    pe.wait_ge(max_ready, 16 * i + x + 1)
                    if there(k, 5):
                        pe.wait_ge(rel_saved, 16 * i + k + 6)
                    wait(pe, row_saved, 16 * i + x)
                    pe.matmul(max_row, negmax[:, x % 4:x % 4 + 1], ident, start=True, stop=True).then_inc(row_ready, 1)
                if there(k, 3):
                    x = k + 3
                    tile_i = x % NB
                    if x % NB == 0:
                        pe.wait_ge(k_loaded[slot(x)], 64 * i + 64 * (x // 16) + 64)
                    wait(pe, max_ready, 16 * i + x)
                    pe.wait_ge(hi_ready, 16 * i + x + 1)
                    for g in range(2):
                        rows = slice(64 * g, 64 * g + K3)
                        j0, j1 = 4 * g, 4 * g + 4
                        edge = min(max(tile_i + 2, j0), j1)
                        for kv, a, b in ((ks[1], edge, j1), (ks[0], j0, edge)):
                            if a < b:
                                ins = pe.matmul(s_ps[:, a * P:b * P], qs[rows, slot(x), tile_i * P:(tile_i + 1) * P],
                                                kv[rows, slot(x), (a - j0) * P:(b - j0) * P], start=True, stop=True)
                        a, b = max(tile_i - 1, j0), min(tile_i + 2, j1)
                        if a < b:
                            c = (a - tile_i + 1) * P
                            ins = pe.matmul(s_ps[:, a * P:b * P], ident_b[:], rel_part[0][:, x % 8, c:c + (b - a) * P],
                                            start=False, stop=True, skip_group_check=True)
                    ins.then_inc(s_ready, 1)
                if there(k):
                    even = k % NB - k % 2
                    if k % 2 == 0:
                        pe.wait_ge(row_saved, 16 * i + k + 2)
                        pe.wait_ge(lo_ready, 16 * i + k + 2)
                    pe.wait_ge(exp_done, 16 * i + k + 1)
                    g = k % 2
                    rows = slice(64 * g, 64 * g + MROW + 1)
                    for j in range(4 * g, 4 * g + 4):
                        both = [(0, 1), (1, 2)] if j == even + 2 else [(0, 2)]
                        band = [h for h in range(2) if abs(j - even - h) <= 1]
                        at = j % 4 * 2
                        for a, b in both:
                            kv = ks[0] if j <= even + b else ks[1]
                            ins = pe.matmul(st[k % 2][:, (at + a) * P:(at + b) * P], kv[rows, slot(k), j % 4 * P:(j % 4 + 1) * P],
                                            qs[rows, slot(k), (even + a) * P:(even + b) * P], start=True, stop=True)
                        for h in band:
                            c = (j - even - h + 1) * P
                            for part in rel_part:
                                ins = pe.matmul(st[k % 2][:, (at + h) * P:(at + h + 1) * P], part[:, (k - k % 2 + h) % 8, c:c + P], ident_b[:],
                                                start=False, stop=True, skip_group_check=True)
                    ins.then_inc(st_ready, 1)
                if there(k, 6):
                    x = k + 6
                    if x % NB == 0:
                        pe.wait_ge(q_loaded[slot(x)], 32 * i + 32 * (x // 16) + 32)
                    wait(pe, rel_saved, 16 * i + x)
                    wait(pe, row_saved, 16 * i + x - 3)
                    q = qs[0:K3, slot(x), x % NB * P:(x % NB + 1) * P]
                    pe.matmul(rel_ps[:, 0:BAND], q, emb_all[:], start=True, stop=True).then_inc(rel_ready, 1)
                if k >= 4:
                    batch, r = k // 4 - 1, k % 4
                    if r == 0:
                        pe.wait_ge(exp_done, 16 * i + k + 2)
                        pe.wait_ge(v_ready, 2 * i + batch // 2 + 1)
                        pe.wait_ge(y_saved, 4 * i + batch + 1)
                    for j in (2 * r, 2 * r + 1):
                        for q in range(4):
                            ins = pe.matmul(acc[32 * q:32 * q + 32, 0:P], vs[:, batch // 2 % 2, j, :],
                                            probs[:, (4 * batch + q - q % 2 + j // 4) % 8, (j % 4 * 2 + q % 2) * P:(j % 4 * 2 + q % 2 + 1) * P],
                                            start=(j == 0), stop=(j == NB - 1))
                    ins.then_inc(pv_done, 1)

            pipeline(pe, one)
            pe.wait_ge(exp_done, BLOCKS + 2)
            weights_turned(router, sb, pe, banks)

        @block.scalar
        def _(act):
            act.sem_inc(exp_done, 2)

            def one(i, k):
                if there(k, 4):
                    x = k + 4
                    act.wait_ge(rel_read[x % 4], 64 * i + 16 * (x // 4) + 16)
                    wait(act, st_ready, 16 * i + x - 7)
                    act.activation(rel_part[0][:, x % 8, :], rel_raw[:, x % 4, :], ACT.Copy).then_inc(hi_ready, 1)
                if there(k):
                    act.wait_ge(st_ready, 16 * i + k + 1)
                    wait(act, pv_done, 16 * i + 4 * (k // 4))
                    act.activation(probs[:, k % 8, :], st[k % 2][:], ACT.Exp, scale=SCALE).then_inc(exp_done, 1)

            pipeline(act, one)
            weights_hi(router, sb, act, banks)

        @block.vector
        def _(dve):
            PIECES = 3
            count = [0]

            def then(ins):
                count[0] += 1
                ins.then_inc(step, 1)
                dve.wait_ge(step, count[0])

            dve.sem_inc(y_saved, 1)
            dve.sem_inc(pv_done, 4)
            for s in range(2):
                dve.sem_inc(y_stored[s], 16)
            dve.tensor_copy(ident_b[:], ident).then_inc(emb_ready, 1)
            dve.wait_ge(cleared, 3)
            for t_ in ks:
                for g in range(2):
                    ins = dve.memset(f32(t_[64 * g + MROW:64 * g + MROW + 1, :, :]), 1.0)
            ins.then_inc(cleared, 1)
            dve.wait_ge(loaded, 48)
            then(dve.tensor_scalar(emb[:, 1, :], emb[:, 0, :], ecol[:, 0:1], None, ALU.subtract))
            then(dve.tensor_copy(emb_hi[:], emb[:, 1, :]))
            then(dve.tensor_tensor(emb[:, 2, :], emb[:, 1, :], f32(emb_hi[:]), ALU.subtract))
            then(dve.tensor_scalar(emb[:, 2, :], emb[:, 2, :], ecol[:, 1:2], None, ALU.mult))
            dve.scalar_tensor_tensor(emb_all[:], f32(emb_hi[:]), ecol[:, 2:3], emb[:, 2, :], ALU.mult, ALU.add).then_inc(emb_ready, 1)

            choosing = choose(router, sb, dve, then, router.biased)

            def one(i, k):
                if 0 <= k < 4 or k >= BLOCKS - 12:
                    for _ in range(PIECES):
                        next(choosing, None)
                if there(k, 2):
                    x = k + 2
                    dve.wait_ge(row_ready, 16 * i + x + 1)
                    for g in range(2):
                        row = 64 * g + MROW
                        ins = dve.tensor_copy(qs[row:row + 1, slot(x), x % NB * P:(x % NB + 1) * P], max_row)
                    ins.then_inc(row_saved, 1)
                if there(k, 3):
                    x = k + 3
                    dve.wait_ge(rest_ready, 16 * i + x + 1)
                    dve.tensor_copy(rel_part[1][:, x % 8, :], rel_rest[:, x % 4, :]).then_inc(mid_ready, 1)
                if there(k, 3):
                    x = k + 3
                    dve.wait_ge(s_ready, 16 * i + x + 1)
                    dve.tensor_reduce(negmax[:, x % 4:x % 4 + 1], s_ps[:], AX.X, ALU.max, negate=True).then_inc(max_ready, 1)
                if there(k, 6):
                    x = k + 6
                    dve.wait_ge(rel_ready, 16 * i + x + 1)
                    wait(dve, rel_written[x % 4], 64 * i + 16 * (x // 4))
                    dve.tensor_copy(rel_sb[:, x % 4, :], rel_ps[:, 0:BAND]).then_inc(rel_saved, 1)
                if k >= 4 and k % 4 == 3:
                    batch = k // 4 - 1
                    dve.wait_ge(pv_done, 16 * i + 4 * batch + 4 + 4)
                    dve.wait_ge(y_stored[batch % 2], 128 * i + 64 * (batch // 2) + 16)
                    dve.tensor_copy(ys[:, batch % 2, :], acc[:, 0:P]).then_inc(y_saved, 1)

            pipeline(dve, one)
            for _ in choosing:
                pass
            weights_lo(router, sb, dve, banks)


def experts(nc, d, sb, scr, layer):
    k = layer.index
    E, CK = layer.E, layer.chunks
    K = len(CK)
    R = layer.rows
    with ExitStack() as ctx:
        def tile(name, shape, dt=F32):
            return ctx.enter_context(nc.sbuf_tensor(f"f{k}_{name}", shape, dt))

        def sem(name):
            return ctx.enter_context(nc.semaphore(f"f{k}_{name}"))

        GRP = 3
        starts = [0, 1, *range(3, K, GRP), K]
        groups = list(zip(starts, starts[1:]))
        raw = tile("raw", [P, 2, 4, GRP * P])
        wide = K * P
        w_hi = [tile(f"w{m}_hi", [P, wide], F32R) for m in (1, 3, 2)]
        w_lo = [tile(f"w{m}_lo", [P, wide], F32R) for m in (1, 3, 2)]
        sel = tile("sel", [P, wide], F32R)
        if k == 0:
            b1, b3 = tile("b1", [P, K]), tile("b3", [P, K])
            b2 = tile("b2", [P, D]); b2_hi = tile("b2_hi", [P, D], F32R); b2_lo = tile("b2_lo", [P, D], F32R)
        gate = tile("gate", [P, 2, CH]); up = tile("up", [P, 2, CH]); hid = tile("hid", [P, 2, CH])
        hid_hi = tile("hid_hi", [P, 4, CH], F32R); hid_lo = tile("hid_lo", [P, 4, CH], F32R)
        if k == 1:
            yv, ysum = sb["xn"], sb["v"]
            y_hi, y_lo = tile("y_hi", [P, N], F32R), tile("y_lo", [P, N], F32R)
            wp = tile("wp", [P, D]); wp_hi = tile("wp_hi", [P, D], F32R); wp_lo = tile("wp_lo", [P, D], F32R)
        else:
            yv = tile("yv", [P, N])
        yT = sb["yT"]

        def pb(name):
            return ctx.enter_context(nc.psum_tensor(f"f{k}_{name}", [P, CH], F32))
        g_ps, u_ps, c_ps = [pb(f"g{i}") for i in range(2)], [pb(f"u{i}") for i in range(2)], [pb(f"c{i}") for i in range(2)]
        y_ps, z_ps = pb("y"), pb("z")

        raw_loaded = [sem(f"raw_loaded{s}") for s in range(2)]
        raw_hi, raw_lo, w_ready = sem("raw_hi"), sem("raw_lo"), sem("w_ready")
        small, att_sorted, att_loaded, att_ready, step = sem("small"), sem("att_sorted"), sem("att_loaded"), sem("att_ready"), sem("step")
        bias_ready, quotient_step = sem("bias_ready"), sem("quotient_step")
        g_ready, u_ready, gate_ready, up_ready, hid_ready = sem("g_ready"), sem("u_ready"), sem("gate_ready"), sem("up_ready"), sem("hid_ready")
        hi_ready, lo_ready, down_done = sem("hi_ready"), sem("lo_ready"), sem("down_done")
        y_ready, turned, out_ready, out_stored = sem("y_ready"), sem("turned"), sem("out_ready"), sem("out_stored")
        names = [("w1", 0), ("w3", 1), ("w2", 2), ("sel", 3)]
        block = ctx.enter_context(nc.Block())

        def pieces(m, c0, c1):
            if m != 2:
                return [(P, c0 * P, min(c1 * P, R))]
            full = R // P
            parts = [(P, c0 * P, min(c1, full) * P), (R - full * P, max(c0, full) * P, c1 * P)]
            return [p for p in parts if p[2] > p[1]]

        @block.sync
        def _(sp):
            if k == 0:
                sp.dma_start(b1[:], d["b1"]).then_inc(small, 16)
                sp.dma_start(b3[:], d["b3"]).then_inc(small, 16)
                sp.dma_start(b2[0:E + 1, :], d["b2"]).then_inc(small, 16)
                sp.dma_start(b2[LO_ROW:LO_ROW + E + 1, :], d["b2"]).then_inc(small, 16)
                sp.dma_start(yv[:].rearrange("p (b t) -> p b t", b=B), scr["y0"]).then_inc(att_loaded, 16)
            else:
                sp.dma_start(wp[:], d["wproj"]).then_inc(small, 16)

            def load(n):
                c0, c1 = groups[n]
                s = n % 2
                if n >= 2:
                    sp.wait_ge(raw_lo, n - 1)
                for name, m in names:
                    for rows, a, b in pieces(m, c0, c1):
                        dst = raw[0:rows, s, m, a - c0 * P:b - c0 * P]
                        if m == 2:
                            sp.dma_start(dst.rearrange("p (c n) -> p c n", n=D),
                                         d[f"w2_{k}"][a:a + (b - a) // P * rows].rearrange("(c p) n -> p c n", p=rows)).then_inc(raw_loaded[s], 16)
                        else:
                            sp.dma_start(dst, d[f"{name}_{k}"][:, a:b]).then_inc(raw_loaded[s], 16)

            load(0)
            load(1)
            if k == 1:
                for w in range(2):
                    for b in range(B):
                        sp.dma_start(scr["y1c"][w, b], scr["y1"][w, b]).then_inc(att_sorted, 16)
                sp.wait_ge(att_sorted, 64)
                for w, t_ in enumerate((yv, ysum)):
                    sp.dma_start(flat(t_).rearrange("p (b t) -> p b t", b=B), scr["y1r"][w]).then_inc(att_loaded, 16)
            for n in range(2, len(groups)):
                load(n)
            if k == 1:
                for t in range(NC):
                    sp.wait_ge(out_ready, t + 1)
                    sp.dma_start(d["out"].rearrange("(c t p) d -> c p t d", p=P, t=4)[t], sb["x"][:, 4 * t:4 * t + 4, :]).then_inc(out_stored, 16)
                sp.wait_ge(out_stored, 16 * NC)

        def raw_count(n):
            return sum(len(pieces(m, *groups[g])) for g in range(n % 2, n + 1, 2) for m in range(4))

        def split_hi(eng, n, copy):
            c0, c1 = groups[n]
            eng.wait_ge(raw_loaded[n % 2], 16 * raw_count(n))
            for m in range(4):
                for rows, a, b in pieces(m, c0, c1):
                    ins = copy((*w_hi, sel)[m][0:rows, a:b], raw[0:rows, n % 2, m, a - c0 * P:b - c0 * P])
            ins.then_inc(raw_hi, 1)

        def split_lo(eng, n):
            c0, c1 = groups[n]
            eng.wait_ge(raw_hi, n + 1)
            for m in range(3):
                for rows, a, b in pieces(m, c0, c1):
                    ins = eng.tensor_tensor(w_lo[m][0:rows, a:b], raw[0:rows, n % 2, m, a - c0 * P:b - c0 * P],
                                            f32(w_hi[m][0:rows, a:b]), ALU.subtract)
            ins.then_inc(raw_lo, 1)

        @block.tensor
        def _(pe):
            if k == 0:
                pe.wait_ge(bias_ready, 2)
            with pe.Fori(0, NC) as ti:
                cols = bass.ds(ti * CH, CH)

                def rise(c):
                    n, m = ti * K + c, CK[c]
                    ch = slice(c * P, c * P + m)
                    if c in starts:
                        pe.wait_ge(raw_lo, starts.index(c) + 1)
                    pe.wait_ge(gate_ready, ti * K + max(c - 1, 0) + 1)
                    g, u, w = g_ps[c % 2][0:m, :], u_ps[c % 2][0:m, :], c_ps[c % 2][0:m, :]
                    pe.matmul(g, w_hi[0][:, ch], sb["x_hi"][:, cols], start=True, stop=False)
                    pe.matmul(g, w_lo[0][:, ch], sb["x_hi"][:, cols], start=False, stop=False)
                    pe.matmul(g, w_hi[0][:, ch], sb["x_lo"][:, cols], start=False, stop=True).then_inc(g_ready, 1)
                    pe.wait_ge(hid_ready, ti * K + max(c - 1, 0) + 1)
                    pe.matmul(u, w_hi[1][:, ch], sb["x_hi"][:, cols], start=True, stop=False)
                    pe.matmul(u, w_lo[1][:, ch], sb["x_hi"][:, cols], start=False, stop=False)
                    pe.matmul(u, w_hi[1][:, ch], sb["x_lo"][:, cols], start=False, stop=True)
                    pe.matmul(w, sel[:, ch], sb["cw_split"][:, cols], start=True, stop=True).then_inc(u_ready, 1)

                def fall(c):
                    n, m = ti * K + c, CK[c]
                    ch = slice(c * P, (c + 1) * P)
                    pe.wait_ge(hi_ready, n + 1)
                    pe.wait_ge(lo_ready, n + 1)
                    pe.matmul(y_ps[:], w_hi[2][0:m, ch], hid_hi[0:m, c % 4, :], start=(k == 1 and c == 0), stop=False)
                    pe.matmul(y_ps[:], w_lo[2][0:m, ch], hid_hi[0:m, c % 4, :], start=False, stop=False)
                    ins = pe.matmul(y_ps[:], w_hi[2][0:m, ch], hid_lo[0:m, c % 4, :], start=False, stop=(k == 0 and c == K - 1))
                    if k == 1 and c == K - 1:
                        pe.wait_ge(att_ready, ti + 2)
                        pe.matmul(y_ps[:], wp_hi[:], y_hi[:, cols], start=False, stop=False)
                        pe.matmul(y_ps[:], wp_lo[:], y_hi[:, cols], start=False, stop=False)
                        ins = pe.matmul(y_ps[:], wp_hi[:], y_lo[:, cols], start=False, stop=True)
                    ins.then_inc(down_done, 1)

                pe.wait_ge(y_ready, ti + 1)
                if k == 0:
                    pe.matmul(y_ps[:], b2_hi[:], sb["cw_split"][:, cols], start=True, stop=False)
                    pe.matmul(y_ps[:], b2_lo[:], sb["cw_split"][:, cols], start=False, stop=False)
                for c in range(K + 2):
                    if c < K:
                        rise(c)
                    if c >= 2:
                        fall(c - 2)
            if k == 1:
                for t in range(NT):
                    if t % 4 == 0:
                        pe.wait_ge(y_ready, t // 4 + 2)
                    if t >= 8 and t % 4 == 0:
                        pe.wait_ge(out_ready, t // 4 - 1)
                    out = (z_ps, g_ps[0])[t // 4 % 2]
                    ins = pe.transpose(out[:, (t % 4) * P:(t % 4 + 1) * P], yT[:, t * P:(t + 1) * P], sb["const"][:, C_ID:C_ID + P])
                    if t % 4 == 3:
                        ins.then_inc(turned, 1)

        @block.scalar
        def _(act):
            def split(n):
                split_hi(act, n, lambda o, x: act.activation(o, x, ACT.Copy))

            def token_tile(ti, first=False):
                for c in range(K + 1):
                    if first and c in starts[:-3]:
                        split(starts.index(c) + 2)
                    n = ti * K + c
                    if c < K:
                        m = CK[c]
                        act.wait_ge(g_ready, n + 1)
                        act.wait_ge(hid_ready, ti * K + max(c - 1, 0) + 1)
                        bias = {"bias": b1[0:m, c:c + 1]} if k == 0 else {}
                        act.activation(gate[0:m, c % 2, :], g_ps[c % 2][0:m, :], ACT.Silu, **bias).then_inc(gate_ready, 1)
                    if c >= 1:
                        c_ = c - 1
                        m = CK[c_]
                        act.wait_ge(hid_ready, ti * K + c_ + 2)
                        act.wait_ge(down_done, ti * K + max(c_ - 3, 0) + 1)
                        act.activation(hid_hi[0:m, c_ % 4, :], hid[0:m, c_ % 2, :], ACT.Copy).then_inc(hi_ready, 1)

            split(0)
            split(1)
            act.sem_inc(gate_ready, 1)
            if k == 0:
                act.wait_ge(small, 64)
            token_tile(0, first=True)
            with act.Fori(1, NC) as ti:
                token_tile(ti)

        @block.gpsimd
        def _(pool):
            def token_tile(ti, first=False):
                for c in range(K):
                    if first and c in starts[:-3]:
                        split_lo(pool, starts.index(c) + 2)
                    m = CK[c]
                    pool.wait_ge(hi_ready, ti * K + c + 1)
                    pool.tensor_tensor(hid_lo[0:m, c % 4, :], hid[0:m, c % 2, :], f32(hid_hi[0:m, c % 4, :]), ALU.subtract).then_inc(lo_ready, 1)

            split_lo(pool, 0)
            split_lo(pool, 1)
            token_tile(0, first=True)
            with pool.Fori(1, NC) as ti:
                token_tile(ti)

        @block.vector
        def _(dve):
            count = [0]

            def then(ins):
                count[0] += 1
                ins.then_inc(step, 1)
                dve.wait_ge(step, count[0])

            dve.sem_inc(hid_ready, 1)
            dve.sem_inc(y_ready, 1)
            dve.sem_inc(down_done, 1)
            if k == 0:
                then(dve.memset(b2_lo[:].bitcast(F32), 0.0))
                dve.wait_ge(small, 64)
                then(dve.memset(b2_hi[:].bitcast(F32), 0.0))
                for rows in (slice(0, E + 1), slice(LO_ROW, LO_ROW + E + 1)):
                    then(dve.tensor_copy(b2_hi[rows, :], b2[rows, :]))
                    dve.tensor_tensor(b2_lo[rows, :], b2[rows, :], f32(b2_hi[rows, :]), ALU.subtract).then_inc(bias_ready, 1)
                dve.wait_ge(att_loaded, 16)
            else:
                dve.wait_ge(small, 16)
                then(dve.tensor_copy(wp_hi[:], wp[:]))
                dve.tensor_tensor(wp_lo[:], wp[:], f32(wp_hi[:]), ALU.subtract).then_inc(att_ready, 1)
            with dve.Fori(0, NC) as ti:
                cols = bass.ds(ti * CH, CH)
                quotient = [
                    lambda: dve.reciprocal(ysum[:, cols], ysum[:, cols]),
                    lambda: dve.tensor_tensor(flat(yv)[:, cols], flat(yv)[:, cols], ysum[:, cols], ALU.mult),
                    lambda: dve.tensor_copy(y_hi[:, cols], flat(yv)[:, cols]),
                    lambda: dve.tensor_tensor(y_lo[:, cols], flat(yv)[:, cols], f32(y_hi[:, cols]), ALU.subtract)]
                for c in range(K):
                    n, m = ti * K + c, CK[c]
                    dve.wait_ge(u_ready, n + 1)
                    dve.wait_ge(gate_ready, n + 2)
                    u, w, g = u_ps[c % 2][0:m, :], c_ps[c % 2][0:m, :], gate[0:m, c % 2, :]
                    if k == 0:
                        dve.scalar_tensor_tensor(up[0:m, c % 2, :], u, b3[0:m, c:c + 1], g, ALU.add, ALU.mult).then_inc(up_ready, 1)
                    else:
                        dve.tensor_tensor(up[0:m, c % 2, :], u, g, ALU.mult).then_inc(up_ready, 1)
                    dve.wait_ge(up_ready, n + 1)
                    if c >= 2:
                        dve.wait_ge(lo_ready, ti * K + c - 1)
                    dve.tensor_tensor(hid[0:m, c % 2, :], w, up[0:m, c % 2, :], ALU.mult).then_inc(hid_ready, 1)
                    if k == 1 and K - 6 <= c < K - 2:
                        at = c - (K - 6)
                        if at == 0:
                            dve.wait_ge(att_loaded, 32)
                        else:
                            dve.wait_ge(quotient_step, ti * 3 + at)
                        quotient[at]().then_inc(quotient_step if at < 3 else att_ready, 1)
                dve.wait_ge(down_done, ti * K + K + 1)
                if k == 0:
                    dve.tensor_tensor(yT[:, cols], y_ps[:], yv[:, cols], ALU.add).then_inc(y_ready, 1)
                else:
                    dve.tensor_copy(yT[:, cols], y_ps[:]).then_inc(y_ready, 1)
            if k == 1:
                for c in range(NC):
                    dve.wait_ge(turned, c + 1)
                    part = sb["x"][:, 4 * c:4 * c + 4, :]
                    bank = (z_ps, g_ps[0])[c % 2]
                    dve.tensor_tensor(part, bank[:].rearrange("p (t d) -> p t d", d=D), part, ALU.add).then_inc(out_ready, 1)


def two_layers(nc, d):
    with ExitStack() as ctx:
        def tile(name, shape, dt=F32):
            return ctx.enter_context(nc.sbuf_tensor(name, shape, dt))

        sb = {
            "const": tile("const", [P, C_ALL]),
            "x": tile("x", [P, NT, D]), "xn": tile("xn", [P, NT, D]),
            "x_hi": tile("x_hi", [P, N], F32R), "x_lo": tile("x_lo", [P, N], F32R),
            "v": tile("v", [P, N]),
            "cw_split": tile("cw_split", [P, N], F32R),
            "yT": tile("yT", [P, N]),
        }
        scr = {}
        for name in ("q0", "k0", "q1", "ka", "kb"):
            whole = nc.dram_tensor("scr_" + name, (TERMS, B, P, T), F32, kind="Internal").ap()
            scr[name] = whole.rearrange("w b p t -> w p b t")
            scr[name + "h"] = whole.rearrange("w b (h r) t -> w (b h) r t", r=HD)
        y0 = nc.dram_tensor("scr_y0", (B * H, HD, T), F32, kind="Internal").ap()
        scr["y0h"] = y0
        scr["y0"] = y0.rearrange("(b h) r t -> (h r) b t", b=B)
        y1 = nc.dram_tensor("scr_y1", (B * H, 2 * HD, T), F32, kind="Internal").ap()
        scr["y1s"] = y1
        scr["y1"] = y1.rearrange("(b h) (w r) t -> w b h r t", b=B, w=2)
        y1c = nc.dram_tensor("scr_y1c", (2, B, H, HD, T), F32, kind="Internal").ap()
        scr["y1c"] = y1c
        scr["y1r"] = y1c.rearrange("w b h r t -> w (h r) b t")
        scr["rel"] = nc.dram_tensor("scr_rel", (16, P, RELROW), F32, kind="Internal").ap()

        with ExitStack() as stage:
            router = Router(nc, stage, L0)
            prepare(nc, d, sb, scr, router)
            sigmoid_attention(nc, d, sb, scr, router)
        experts(nc, d, sb, scr, L0)
        with ExitStack() as stage:
            router = Router(nc, stage, L1)
            prepare(nc, d, sb, scr, router)
            softmax_attention(nc, d, sb, scr, router)
        experts(nc, d, sb, scr, L1)


def selection(layer, np):
    sel = np.zeros((P, layer.rows), np.float32)
    per = 64 if layer.index == 0 else 176
    for r in range(layer.rows):
        e = min(r // per, layer.E)
        sel[e, r] = sel[LO_ROW + e, r] = 1.0
    return sel


def constants(np):
    c = np.zeros((P, C_ALL), np.float32)
    c[:, C_ID:C_ID + P] = np.eye(P)
    c[:, C_CAUSAL:C_CAUSAL + P] = np.triu(np.ones((P, P)))
    c[:, C_IOTA:C_IOTA + 32] = np.arange(32)
    c[:, C_TRI8:C_TRI8 + 64] = np.tril(np.ones((8, 8)), -1).ravel()
    c[:, C_TRI4:C_TRI4 + 16] = np.tril(np.ones((4, 4)), -1).ravel()
    c[:, C_POW:C_POW + NT] = -0.5
    return c


def laid_out(inputs, np):
    a = {n: np.asarray(v) for n, v in inputs.items()}
    pos = a["L1_attn_pos_emb_k"]
    by_offset = np.concatenate([pos[RADIUS:], pos[:RADIUS], np.repeat(pos[RADIUS - 1:RADIUS], P, 0)]).T
    rows24 = np.zeros((TERMS * HD, 4), np.float32)
    rows24[:, 0] = np.tile(pos[RADIUS], TERMS)
    rows24[2 * HD:, 1] = 1.0
    rows24[:2 * HD, 2] = 1.0
    out = {
        "const": constants(np),
        "x": a["L0_attn_x"].reshape(N, D),
        "gw0": a["L0_ffn_gw"], "gb0": a["L0_ffn_gb"],
        "gw1": a["L1_ffn_gate_w"].T, "gb1": a["L1_ffn_gate_bias"],
        "bqk": np.stack([a["L0_attn_bv_q"].ravel(), a["L0_attn_bv_k"].ravel()], 1),
        "bv": a["L0_attn_bv_v"].ravel(),
        "w1_0": np.concatenate([a["L0_ffn_w1"].transpose(1, 0, 2).reshape(D, -1), a["L0_ffn_sw1"]], 1),
        "w3_0": np.concatenate([a["L0_ffn_w3"].transpose(1, 0, 2).reshape(D, -1), a["L0_ffn_sw3"]], 1),
        "w2_0": np.concatenate([a["L0_ffn_w2"].reshape(-1, D), a["L0_ffn_sw2"]]),
        "b1": np.concatenate([a["L0_ffn_b1"].ravel(), a["L0_ffn_sb1"]]).reshape(-1, P).T,
        "b3": np.concatenate([a["L0_ffn_b3"].ravel(), a["L0_ffn_sb3"]]).reshape(-1, P).T,
        "b2": np.concatenate([a["L0_ffn_b2"], a["L0_ffn_sb2"][None]]),
        "w1_1": np.concatenate([a["L1_ffn_gate_proj"].reshape(-1, D), a["L1_ffn_shared_gate_w"]]).T,
        "w3_1": np.concatenate([a["L1_ffn_up_proj"].reshape(-1, D), a["L1_ffn_shared_up_w"]]).T,
        "w2_1": np.concatenate([a["L1_ffn_down_proj"].transpose(0, 2, 1).reshape(-1, D), a["L1_ffn_shared_down_w"].T]),
        "sel_0": selection(L0, np), "sel_1": selection(L1, np),
        "wqkv": np.stack([a["L1_attn_Wq"].T, a["L1_attn_Wk"].T, a["L1_attn_Wv"].T], 1),
        "wproj": a["L1_attn_Wproj"].T,
        "ecol": np.stack([np.tile(pos[RADIUS], H), np.tile(pos[RADIUS - 1], H)], 1),
        "emb": np.tile(by_offset, (TERMS, 1)),
        "ecol24": rows24,
    }
    return {n: np.ascontiguousarray(v) for n, v in out.items()}


def kernel(**inputs):
    import numpy as _np
    import concourse.bacc as _bacc
    from concourse.bass_utils import run_bass_kernel_spmd as _run

    nc = _bacc.Bacc("TRN2", target_bir_lowering=False, num_devices=1)
    arrays, d = {}, {}
    for name, a in laid_out(inputs, _np).items():
        arrays[f"in_{name}"] = a
        d[name] = nc.dram_tensor(f"in_{name}", a.shape, mybir.dt.from_np(a.dtype), kind="ExternalInput").ap()
    d["out"] = nc.dram_tensor("out_0", (N, D), F32, kind="ExternalOutput").ap()
    two_layers(nc, d)
    r = _run(nc, [arrays], core_ids=[0])
    return r.results[0]["out_0"].reshape(B, T, D)
```
